# Optimizing a Trainium2 kernel written in Bass

```python
import numpy as np
import jax
import jax.numpy as jnp

def _softmax(x, axis=-1):
    return jax.nn.softmax(x, axis=axis)

def _gelu(x):
    return jax.nn.gelu(x, approximate=True)

def _silu(x):
    return jax.nn.silu(x)

def _sigmoid(x):
    return jax.nn.sigmoid(x)

def _layernorm(x, axis=-1, eps=1e-05):
    m = jnp.mean(x, axis=axis, keepdims=True)
    v = jnp.var(x, axis=axis, keepdims=True)
    return (x - m) / jnp.sqrt(v + eps)

def _scatter_add(tgt, idx, src, axis=0):
    return tgt.at[idx].add(src)

def _segment_sum(src, seg, n):
    return jax.ops.segment_sum(src, seg, n)
kernel_name = 'mk_adj_preln_d2_adj_r2_5af60e'

def setup_inputs(seed: int=0):
    np.random.seed(seed)
    _w = jnp.asarray

    def _rec_inputs():
        import jax
        import jax.numpy as jnp
        _gk = jax.random.key(seed)
        x = -0.000125 + 0.9999 * jax.random.normal(jax.random.fold_in(_gk, 1), (8, 1024, 128), jnp.float32)
        _a = jax.random.bernoulli(jax.random.fold_in(_gk, 2), 0.0078125, (1024, 1024))
        _a = jnp.logical_or(_a, jnp.swapaxes(_a, -1, -2))
        _a = jnp.logical_or(_a, jnp.eye(1024, dtype=bool))
        _af = _a.astype(jnp.float32)
        _af = _af * jax.random.uniform(jax.random.fold_in(_gk, 3), (1024, 1024), jnp.float32, 0.05, 0.000488281)
        adj = _af
        return (x, adj)
    x, adj = _rec_inputs()

    def _L0_gnn_setup():
        import jax, jax.numpy as jnp
        import numpy as np
        B, T, D, H = (64, 1024, 128, 128)
        MAX_SKIP = 4

        def _lstm_last(Wih, Whh, bih, bhh, xs):
            N, _, Hd = xs.shape
            bias = bih + bhh

            def step(carry, x_t):
                h, c = carry
                g = x_t @ Wih.T + h @ Whh.T + bias
                i, f, gg, o = jnp.split(g, 4, axis=-1)
                c = jax.nn.sigmoid(f) * c + jax.nn.sigmoid(i) * jnp.tanh(gg)
                h = jax.nn.sigmoid(o) * jnp.tanh(c)
                return ((h, c), None)
            init = (jnp.zeros((N, Hd), xs.dtype), jnp.zeros((N, Hd), xs.dtype))
            (h_last, _), _ = jax.lax.scan(step, init, jnp.swapaxes(xs, 0, 1))
            return h_last
        key = jax.random.key(seed)
        ks = jax.random.split(key, 8)
        s = 0.05
        x = jax.random.normal(ks[0], (B, T, D), jnp.float32)
        adj = jax.random.uniform(ks[1], (T, T), jnp.float32) / T
        Wg0 = jax.random.normal(ks[2], (D, H), jnp.float32) * s
        bg0 = jnp.zeros((H,), jnp.float32)
        Wg1 = jax.random.normal(ks[3], (H, H), jnp.float32) * s
        bg1 = jnp.zeros((H,), jnp.float32)
        Wih = jax.random.normal(ks[4], (MAX_SKIP, 4 * H, H), jnp.float32) * s
        Whh = jax.random.normal(ks[5], (MAX_SKIP, 4 * H, H), jnp.float32) * s
        bih = jax.random.normal(ks[6], (MAX_SKIP, 4 * H), jnp.float32) * s
        bhh = jax.random.normal(ks[7], (MAX_SKIP, 4 * H), jnp.float32) * s
        return dict(x=x, adj=adj, Wg0=Wg0, bg0=bg0, Wg1=Wg1, bg1=bg1, Wih=Wih, Whh=Whh, bih=bih, bhh=bhh)
    _L0_gnn_all = _L0_gnn_setup()
    _L0_gnn_in = {k: v for k, v in _L0_gnn_all.items() if k in ('Wg0', 'bg0', 'Wg1', 'bg1', 'Wih', 'Whh', 'bih', 'bhh')}
    del _L0_gnn_all

    def _L1_gnn_setup():
        import jax, jax.numpy as jnp
        import numpy as np
        EPS = 1e-05

        def _batchnorm(x, gamma, beta):
            mu = jnp.mean(x, axis=0)
            var = jnp.var(x, axis=0)
            return (x - mu) * jax.lax.rsqrt(var + EPS) * gamma + beta
        key = jax.random.key(seed)
        ks = jax.random.split(key, 4)
        b, n, d, h, o = (32, 1024, 128, 256, 128)
        features = jax.random.normal(ks[0], (b, n, d), dtype=jnp.float32)
        A = jax.random.uniform(ks[1], (n, n), dtype=jnp.float32)
        lim1 = float(np.sqrt(6.0 / (d + h)))
        W1 = jax.random.uniform(ks[2], (h, d), minval=-lim1, maxval=lim1, dtype=jnp.float32)
        b1 = jnp.zeros((h,), jnp.float32)
        lim2 = float(np.sqrt(6.0 / (h + o)))
        W2 = jax.random.uniform(ks[3], (o, h), minval=-lim2, maxval=lim2, dtype=jnp.float32)
        b2 = jnp.zeros((o,), jnp.float32)
        g1 = jnp.ones((h,), jnp.float32)
        be1 = jnp.zeros((h,), jnp.float32)
        g2 = jnp.ones((o,), jnp.float32)
        be2 = jnp.zeros((o,), jnp.float32)
        return {'features': features, 'A': A, 'W1': W1, 'b1': b1, 'g1': g1, 'be1': be1, 'W2': W2, 'b2': b2, 'g2': g2, 'be2': be2}
    _L1_gnn_all = _L1_gnn_setup()
    _L1_gnn_in = {k: v for k, v in _L1_gnn_all.items() if k in ('W1', 'b1', 'g1', 'be1', 'W2', 'b2', 'g2', 'be2')}
    del _L1_gnn_all
    return {'x': x, 'adj': adj, 'L0_gnn_Wg0': _L0_gnn_in['Wg0'], 'L0_gnn_bg0': _L0_gnn_in['bg0'], 'L0_gnn_Wg1': _L0_gnn_in['Wg1'], 'L0_gnn_bg1': _L0_gnn_in['bg1'], 'L0_gnn_Wih': _L0_gnn_in['Wih'], 'L0_gnn_Whh': _L0_gnn_in['Whh'], 'L0_gnn_bih': _L0_gnn_in['bih'], 'L0_gnn_bhh': _L0_gnn_in['bhh'], 'L1_gnn_W1': _L1_gnn_in['W1'], 'L1_gnn_b1': _L1_gnn_in['b1'], 'L1_gnn_g1': _L1_gnn_in['g1'], 'L1_gnn_be1': _L1_gnn_in['be1'], 'L1_gnn_W2': _L1_gnn_in['W2'], 'L1_gnn_b2': _L1_gnn_in['b2'], 'L1_gnn_g2': _L1_gnn_in['g2'], 'L1_gnn_be2': _L1_gnn_in['be2']}

def reference(x, adj, L0_gnn_Wg0, L0_gnn_bg0, L0_gnn_Wg1, L0_gnn_bg1, L0_gnn_Wih, L0_gnn_Whh, L0_gnn_bih, L0_gnn_bhh, L1_gnn_W1, L1_gnn_b1, L1_gnn_g1, L1_gnn_be1, L1_gnn_W2, L1_gnn_b2, L1_gnn_g2, L1_gnn_be2):
    import jax
    import jax.numpy as jnp

    def _L0_gnn_ref(x, adj, Wg0, bg0, Wg1, bg1, Wih, Whh, bih, bhh):
        import jax, jax.numpy as jnp
        import numpy as np
        B, T, D, H = (64, 1024, 128, 128)
        MAX_SKIP = 4

        def _lstm_last(Wih, Whh, bih, bhh, xs):
            N, _, Hd = xs.shape
            bias = bih + bhh

            def step(carry, x_t):
                h, c = carry
                g = x_t @ Wih.T + h @ Whh.T + bias
                i, f, gg, o = jnp.split(g, 4, axis=-1)
                c = jax.nn.sigmoid(f) * c + jax.nn.sigmoid(i) * jnp.tanh(gg)
                h = jax.nn.sigmoid(o) * jnp.tanh(c)
                return ((h, c), None)
            init = (jnp.zeros((N, Hd), xs.dtype), jnp.zeros((N, Hd), xs.dtype))
            (h_last, _), _ = jax.lax.scan(step, init, jnp.swapaxes(xs, 0, 1))
            return h_last
        h = jax.nn.relu(jnp.einsum('ts,bsh->bth', adj, x @ Wg0 + bg0))
        h = jax.nn.relu(jnp.einsum('ts,bsh->bth', adj, h @ Wg1 + bg1))
        Bv, Tv, Hd = h.shape
        for p in range(1, MAX_SKIP + 1):
            nw = Tv // p
            wins = h[:, :nw * p, :].reshape(Bv * nw, p, Hd)
            last = _lstm_last(Wih[p - 1], Whh[p - 1], bih[p - 1], bhh[p - 1], wins)
            idx = jnp.arange(nw) * p + (p - 1)
            h = h.at[:, idx, :].set(last.reshape(Bv, nw, Hd))
        return h

    def _L1_gnn_ref(features, A, W1, b1, g1, be1, W2, b2, g2, be2):
        import jax, jax.numpy as jnp
        import numpy as np
        EPS = 1e-05

        def _batchnorm(x, gamma, beta):
            mu = jnp.mean(x, axis=0)
            var = jnp.var(x, axis=0)
            return (x - mu) * jax.lax.rsqrt(var + EPS) * gamma + beta
        b, n, d = features.shape
        A_norm = A + jnp.eye(n, dtype=A.dtype)
        deg = jnp.sum(A_norm, axis=0) + jnp.sum(A_norm, axis=1) - jnp.diagonal(A_norm)
        dinv = jax.lax.rsqrt(deg)
        A_hat = A_norm * dinv[:, None] * dinv[None, :]
        agg = jnp.einsum('nm,bmd->bnd', A_hat, features)
        x = agg.reshape(-1, d)
        h = jax.nn.relu(_batchnorm(x @ W1.T + b1, g1, be1))
        out = h @ W2.T + b2
        out = _batchnorm(out, g2, be2)
        return out.reshape(b, n, -1)
    h = jnp.maximum(_layernorm(x, axis=-1), 0.0)
    x = x + _L0_gnn_ref(h, adj, L0_gnn_Wg0, L0_gnn_bg0, L0_gnn_Wg1, L0_gnn_bg1, L0_gnn_Wih, L0_gnn_Whh, L0_gnn_bih, L0_gnn_bhh)
    h = jnp.maximum(_layernorm(x, axis=-1), 0.0)
    x = x + _L1_gnn_ref(h, adj, L1_gnn_W1, L1_gnn_b1, L1_gnn_g1, L1_gnn_be1, L1_gnn_W2, L1_gnn_b2, L1_gnn_g2, L1_gnn_be2)
    return x

_drawn_inputs = setup_inputs


def setup_inputs(seed=0):
    import zlib

    import numpy as np

    out = dict(_drawn_inputs(seed))
    spreads = {'L0_gnn_bg0': (0.0, 0.8),
     'L0_gnn_bg1': (0.0, 0.8),
     'L1_gnn_b1': (0.0, 0.8),
     'L1_gnn_g1': (1.0, 0.2),
     'L1_gnn_be1': (0.0, 0.1),
     'L1_gnn_b2': (0.0, 0.8),
     'L1_gnn_g2': (1.0, 0.2),
     'L1_gnn_be2': (0.0, 0.1)}
    factors = {'L0_gnn_Wg0': 8.0, 'L0_gnn_Wg1': 8.0, 'L0_gnn_Wih': 6.115, 'L0_gnn_Whh': 8.0}
    for name, (base, spread) in spreads.items():
        noise = np.random.default_rng([zlib.crc32(name.encode()), seed]).standard_normal(out[name].shape)
        drawn = base * np.exp(spread * noise) if base else spread * noise
        out[name] = jnp.asarray(drawn.astype(out[name].dtype))
    for name, factor in factors.items():
        out[name] = (out[name] * factor).astype(out[name].dtype)
    return out
```

```python
from contextlib import ExitStack

import concourse.bass as bass
from concourse import mybir

ALU = mybir.AluOpType
ACT = mybir.ActivationFunctionType
AX = mybir.AxisListType.X
F32 = mybir.dt.float32
F32R = mybir.dt.float32r

P = 128
B, T, D, H = 8, 1024, 128, 128
F = 256
NT = T // P
CH = 512
NC = T // CH
TPC = CH // P
MAX_SKIP = 4
EPS = 1e-5
GATES = 4
IN, FORGET, CELL, OUT = range(GATES)


class Step:

    def __init__(self, p, s, first_column, windows):
        self.p, self.s, self.first_column, self.windows = p, s, first_column, windows
        self.zero_state = s == 0
        self.ends_windows = s == p - 1
        self.gates = [IN, CELL, OUT] if self.zero_state else [IN, CELL, FORGET, OUT]

    def columns(self, state):
        last = self.first_column + (self.windows - 1) * self.p + 1
        return state[:, self.first_column:last:self.p]


def even(n):
    return n + n % 2


STEPS = [Step(1, 0, c * CH, CH) for c in range(NC)]
for _p in range(2, MAX_SKIP + 1):
    STEPS += [Step(_p, _s, _s, even(T // _p)) for _s in range(_p)]
NS = len(STEPS)
TW = max(even(T // p) * p for p in range(1, MAX_SKIP + 1))
GATE_USES = [(k, g) for k, st in enumerate(STEPS) for g in st.gates]
NG = len(GATE_USES)
RECURRENT = [k for k, st in enumerate(STEPS) if not st.ends_windows]
NR = len(RECURRENT)
RESPLIT = [k for k, st in enumerate(STEPS) if st.ends_windows and st.p < MAX_SKIP]
NX = NC + len(RESPLIT)


def gate_used(k, g):
    return GATE_USES.index((k, g)) + 1


def gate_freed(k, g):
    before = [n for n, (j, gg) in enumerate(GATE_USES) if gg == g and j < k]
    last = max(n for n, (_, gg) in enumerate(GATE_USES) if gg == g)
    return before[-1] + 1 if before else last + 1 - NG


def state_ready(k):
    if k < NC:
        return k + 1
    return NC + sum(j < k and STEPS[j].p < STEPS[k].p for j in RESPLIT)


class Graph:

    def __init__(self, base, loop=None):
        self.base, self.loop = base, loop
        self.index = base if loop is None else loop + base

    def count(self, per, n):
        fixed = self.base * per + n
        return fixed if self.loop is None else self.loop * per + fixed


def wait_past(eng, sem, value):
    if isinstance(value, int) and value <= 0:
        return
    eng.wait_ge(sem, value)


def at_most(value, limit):
    return min(value, limit) if isinstance(value, int) else value


def program(nc, x, adj_t, wg0, wg1, bg0, bg1, wih_t, whh_t, bih_t, bhh_t, w1_t, b1_t, g1_t, be1_t,
            w2_t, b2_t, g2_t, be2_t, ident_in, out):
    scratch = nc.dram_tensor("hidden_scratch", [B, 2, P, T], F32, kind="Internal").ap()
    with ExitStack() as ctx:
        def sb(name, shape, dt=F32):
            return ctx.enter_context(nc.sbuf_tensor(name, shape, dt))

        def sem(name):
            return ctx.enter_context(nc.semaphore(name))

        base = nc.sbuf_base
        base = (base + 31) // 32 * 32
        at = [base]

        def place(name, shape, dt=F32):
            n = 4
            for s in shape[1:]:
                n *= s
            t = nc.alloc_sbuf_tensor_at(name, shape, dt, offset=at[0])
            at[0] += (n + 31) // 32 * 32
            return t

        adj_hi = place("adj_hi", [P, NT, T], F32R)
        adj_lo = place("adj_lo", [P, NT, T], F32R)
        hid = nc.alloc_sbuf_tensor_at("hidden", [P, 2, B, T], F32, offset=base)
        z_at = at[0]
        wih_hi = place("wih_hi", [P, MAX_SKIP, GATES * H], F32R)
        wih_lo = place("wih_lo", [P, MAX_SKIP, GATES * H], F32R)
        whh_hi = place("whh_hi", [P, MAX_SKIP - 1, GATES * H], F32R)
        whh_lo = place("whh_lo", [P, MAX_SKIP - 1, GATES * H], F32R)
        state_hi = place("state_hi", [P, TW], F32R)
        state_lo = place("state_lo", [P, TW], F32R)
        assert at[0] - z_at >= B * T * 4
        z = nc.alloc_sbuf_tensor_at("z", [P, B, T], F32, offset=z_at)
        state = place("state", [P, TW])
        rec = place("rec", [P, CH])
        rec_hi = place("rec_hi", [P, CH], F32R)
        rec_lo = place("rec_lo", [P, CH], F32R)
        gate = place("gate", [P, GATES, CH])
        cell = place("cell", [P, CH])
        cand = place("cand", [P, CH])
        cell_tanh = place("cell_tanh", [P, CH])
        xa = place("xa", [P, B, NT, D])
        norm = place("norm", [P, NT, D])
        feat = place("feat", [P, T])
        h2 = place("h2", [P, T])
        summed = place("summed", [P, T])
        y_hi = place("y_hi", [P, NT, H], F32R)
        y_lo = place("y_lo", [P, NT, H], F32R)
        f_hi = place("f_hi", [P, NT, D], F32R)
        f_lo = place("f_lo", [P, NT, D], F32R)
        agg = place("agg", [P, T])
        hb = place("hb", [P, 4, CH])
        dinv_row = place("dinv_row", [P, T])
        ident = place("ident", [P, P])
        ident_r = place("ident_r", [P, P], F32R)
        ones = place("ones", [P, P])
        ones_r = place("ones_r", [P, P], F32R)
        wg = place("wg", [P, 2, H])
        bg = place("bg", [P, 2, H])
        w1 = place("w1", [P, F])
        w2 = place("w2", [P, 2, D])
        bias_in = place("bias_in", [P, 2, MAX_SKIP * GATES])
        bias = place("bias", [P, MAX_SKIP * GATES])
        bn1 = place("bn1", [P, 3, 2])
        bn2 = place("bn2", [P, 3, 1])
        stats = place("stats", [P, 2, NT, 6])
        moments = place("moments", [P, 2, NT, 2])
        veps = place("veps", [P, 2, NT])
        rstd = place("rstd", [P, 2, NT])
        minus_half = place("minus_half", [P, NT])
        eps = place("eps", [P, NT])
        fence_word = place("fence_word", [P, 8])
        colsum = place("colsum", [P, NT])
        rowsum = place("rowsum", [P, NT])
        diag = place("diag", [P, NT])
        deg = place("deg", [P, 3, NT])
        dinv = place("dinv", [P, NT])
        hstats = place("hstats", [P, 2, B * NC, 6])
        zstats = place("zstats", [P, B * NC, 6])
        bnm = place("bnm", [P, 2, 2])
        bnv = place("bnv", [P, 2])
        bnr = place("bnr", [P, 2])
        bns = place("bns", [P, 2])
        bnt = place("bnt", [P, 2])
        bnu = place("bnu", [P, 2])
        assert at[0] <= nc.sbuf_usable_end, (at[0], nc.sbuf_usable_end)
        adj_stage = [xa[:, n + 1, :, :].rearrange("p a b -> p (a b)") for n in range(NT - 1)] + [h2[:, :]]
        whh_stage = [agg[:, 0:CH], agg[:, CH:T], cand[:, :]]
        wih_stage = [cell_tanh[:, :], cell[:, :], rec[:, :], dinv_row[:, 0:CH]]

        ps = [ctx.enter_context(nc.psum_tensor(f"bank{i}", [P, CH], F32)) for i in range(8)]
        gate_ps = ps[0:4]
        acc = ps[4:6]
        small = ps[6:8]

        adj_in = [sem(f"adj_in{n}") for n in range(NT)]
        consts_in, x_first_in, x_rest_in, wih_in = sem("consts_in"), sem("x_first_in"), sem("x_rest_in"), sem("wih_in")
        consts_set, consts_made = sem("consts_set"), sem("consts_made")
        adj_hi_ready, adj_lo_ready = sem("adj_hi_ready"), sem("adj_lo_ready")
        w_hi_ready, w_lo_ready = sem("w_hi_ready"), sem("w_lo_ready")
        deg_step, rowsum_ps, dinv_diag, dinv_ps, dinv_ready = (
            sem("deg_step"), sem("rowsum_ps"), sem("dinv_diag"), sem("dinv_ps"), sem("dinv_ready"))
        ln_stats, ln_moments, ln_veps, ln_rstd, ln_centred, ln_done = (
            [sem(f"{name}{which}") for which in range(2)]
            for name in ("ln_stats", "ln_moments", "ln_veps", "ln_rstd", "ln_centred", "ln_done"))
        norm_t, feat0 = sem("norm_t"), sem("feat0")
        y_ps, y_summed, y_hi_set, y_lo_set = sem("y_ps"), sem("y_summed"), sem("y_hi_set"), sem("y_lo_set")
        adj0_done, feat1 = sem("adj0_done"), sem("feat1")
        adj1_done, h2_ready = sem("adj1_done"), sem("h2_ready")
        state_hi_set, state_split = sem("state_hi_set"), sem("state_split")
        gate_done, gate_read = sem("gate_done"), sem("gate_read")
        cand_ready, forgot, cell_ready, tanh_ready, h_ready = (
            sem("cand_ready"), sem("forgot"), sem("cell_ready"), sem("tanh_ready"), sem("h_ready"))
        rec_hi_set, rec_split = sem("rec_hi_set"), sem("rec_split")
        state_t, x1_ready = sem("state_t"), sem("x1_ready")
        f_scaled, f_hi_set, f_lo_set = sem("f_scaled"), sem("f_hi_set"), sem("f_lo_set")
        agg_done, agg_scaled = sem("agg_done"), sem("agg_scaled")
        hid_ps, hid_set, hid_stats = sem("hid_ps"), sem("hid_set"), sem("hid_stats")
        hid_stored = [sem(f"hid_stored{n}") for n in range(4)]
        hid_in = [sem(f"hid_in{b}") for b in range(B)]
        bn_step, bn_rstd, bn_own, dinv_step = sem("bn_step"), sem("bn_rstd"), sem("bn_own"), sem("dinv_step")
        bn1_ready, bn2_ready = sem("bn1_ready"), sem("bn2_ready")
        hid_relu, z_ps, z_set, z_stats = sem("hid_relu"), sem("z_ps"), sem("z_set"), sem("z_stats")
        y_set, y_t, y_added, y_stored = sem("y_set"), sem("y_t"), sem("y_added"), sem("y_stored")

        def periods(eng, body):
            def one(j, loop=None):
                body(*(Graph(j - d, loop) if loop is not None or 0 <= j - d < B else None for d in range(-1, 3)))
            for j in range(3):
                one(j)
            with eng.Fori(0, B - 4) as i:
                one(3, i)
            for j in range(B - 1, B + 2):
                one(j)

        block = ctx.enter_context(nc.Block())

        @block.sync
        def _(sp):
            sp.dma_start(xa[:, 0, :, :], x[0].rearrange("(n p) d -> p n d", p=P)).then_inc(x_first_in, 16)
            small_in = [
                (ident[:, :], ident_in), (wg[:, 0, :], wg0), (wg[:, 1, :], wg1),
                (bg[:, 0, :], bg0.broadcast_to([P, H])), (bg[:, 1, :], bg1.broadcast_to([P, H])),
                (w1[:, :], w1_t), (w2[:, :, :], w2_t), (bias_in[:, 0, :], bih_t), (bias_in[:, 1, :], bhh_t),
                (bn1[:, 0, :], b1_t), (bn1[:, 1, :], g1_t), (bn1[:, 2, :], be1_t),
                (bn2[:, 0, :], b2_t), (bn2[:, 1, :], g2_t), (bn2[:, 2, :], be2_t)]
            for dst, src in small_in[:5]:
                sp.dma_start(dst, src).then_inc(consts_in, 16)
            for n in range(NT):
                sp.dma_start(adj_stage[n], adj_t[n * P:(n + 1) * P, :]).then_inc(adj_in[n], 16)
            for dst, src in small_in[5:]:
                sp.dma_start(dst, src).then_inc(consts_in, 16)
            for p in range(MAX_SKIP):
                sp.dma_start(wih_stage[p], wih_t[:, p, :]).then_inc(wih_in, 16)
            for p in range(1, MAX_SKIP):
                sp.dma_start(whh_stage[p - 1], whh_t[:, p, :]).then_inc(wih_in, 16)
            sp.wait_ge(adj_lo_ready, NT)
            sp.wait_ge(deg_step, NT)
            for b in range(1, B):
                sp.dma_start(xa[:, b, :, :], x[b].rearrange("(n p) d -> p n d", p=P)).then_inc(x_rest_in, 16)

            def stage(coming, front, lstm, back):
                if back is None:
                    return
                for c in range(NC):
                    for m in range(2):
                        n = 2 * c + m
                        sp.wait_ge(hid_set, back.count(4, n + 1))
                        sp.dma_start(scratch[back.index, m, :, c * CH:(c + 1) * CH], hb[:, n, :]).then_inc(hid_stored[n], 16)
            periods(sp, stage)
            sp.wait_ge(agg_done, NC * B)
            for n in range(4):
                sp.wait_ge(hid_stored[n], 16 * B)
            for b in range(B):
                sp.dma_start(hid[:, :, b, :], scratch[b].rearrange("m p t -> p m t")).then_inc(hid_in[b], 16)
            with sp.Fori(0, B) as b:
                for c in range(NC):
                    sp.wait_ge(y_added, b * NC + c + 1)
                    sp.dma_start(out[b, c * CH:(c + 1) * CH, :].rearrange("(n p) d -> p n d", p=P),
                                 xa[:, b, c * TPC:(c + 1) * TPC, :]).then_inc(y_stored, 16)
            sp.wait_ge(y_stored, 16 * NC * B)

        @block.gpsimd
        def _(pool):
            pool.memset(ones[:, :], 1.0).then_inc(consts_set, 1)
            pool.memset(ones_r[:, :].bitcast(F32), 1.0).then_inc(consts_set, 1)
            pool.memset(minus_half[:, :], -0.5).then_inc(consts_set, 1)
            pool.memset(eps[:, :], EPS).then_inc(consts_set, 1)
            pool.memset(state_hi[:, T:TW].bitcast(F32), 0.0).then_inc(consts_set, 1)
            pool.memset(state_lo[:, T:TW].bitcast(F32), 0.0).then_inc(consts_set, 1)
            pool.wait_ge(consts_set, 6)

            def layernorm(g, which):
                pool.wait_ge(ln_moments[which], g.count(1, 1))
                pool.tensor_tensor(veps[:, which, :], moments[:, which, :, 1], eps[:, :], ALU.add).then_inc(ln_veps[which], 1)
                mean = moments[:, which, :, 0].unsqueeze(2).broadcast_to([P, NT, D])
                scale = rstd[:, which, :].unsqueeze(2).broadcast_to([P, NT, D])
                if which == 0:
                    wait_past(pool, norm_t, g.count(NC, 0))
                    wait_past(pool, f_lo_set, g.count(1, -2))
                else:
                    wait_past(pool, norm_t, at_most(g.count(NC, 3 * NC), B * NC))
                    wait_past(pool, f_lo_set, g.count(1, 0))
                pool.tensor_tensor(norm[:, :, :], xa[:, g.index, :, :], mean, ALU.subtract).then_inc(ln_centred[which], 1)
                pool.wait_ge(ln_veps[which], g.count(1, 1))
                pool.tensor_tensor(rstd[:, which, :], veps[:, which, :], minus_half[:, :], ALU.pow).then_inc(ln_rstd[which], 1)
                pool.wait_ge(ln_rstd[which], g.count(1, 1))
                pool.wait_ge(ln_centred[which], g.count(1, 1))
                pool.tensor_tensor(norm[:, :, :], norm[:, :, :], scale, ALU.mult).then_inc(ln_done[which], 1)

            pool.wait_ge(x_first_in, 16)
            layernorm(Graph(0), 0)

            def stage(coming, front, lstm, back):
                if front is not None and back is None and front.base == 1:
                    pool.wait_ge(deg_step, NT + 5)
                    pool.tensor_tensor(dinv[:, :], deg[:, 2, :], minus_half[:, :], ALU.pow).then_inc(dinv_diag, 1)
                if back is not None:
                    layernorm(back, 1)
                if coming is not None:
                    layernorm(coming, 0)
            periods(pool, stage)

            for which in range(2):
                pool.wait_ge(bn_step, which + 1)
                pool.tensor_tensor(bnr[:, :], bnv[:, :], minus_half[:, 0:2], ALU.pow).then_inc(bn_rstd, 1)

        @block.scalar
        def _(act):
            for n in range(NT):
                act.wait_ge(adj_in[n], 16)
                act.activation(adj_hi[:, n, :], adj_stage[n], ACT.Identity,
                               accum_out=colsum[:, n:n + 1]).then_inc(adj_hi_ready, 1)

            def gates(g, k):
                st = STEPS[k]
                n = st.windows
                for q in st.gates:
                    act.wait_ge(gate_done, g.count(NG, gate_used(k, q)))
                    wait_past(act, h_ready if q == OUT else cell_ready, g.count(NS, k))
                    act.activation(gate[:, q, 0:n], gate_ps[q][:, 0:n], ACT.Tanh if q == CELL else ACT.Sigmoid,
                                   bias=bias[:, (st.p - 1) * GATES + q:(st.p - 1) * GATES + q + 1]).then_inc(gate_read, 1)
                act.wait_ge(cell_ready, g.count(NS, k + 1))
                act.activation(cell_tanh[:, 0:n], cell[:, 0:n], ACT.Tanh).then_inc(tanh_ready, 1)

            def half(buffer, c):
                return buffer[:, c * CH:(c + 1) * CH]

            def first_features(g, c):
                act.wait_ge(norm_t, g.count(NC, c + 1))
                wait_past(act, y_ps, g.count(2 * NC, 0))
                act.activation(half(feat, c), small[c][:, :], ACT.Relu).then_inc(feat0, 1)

            def second_features(g, c):
                act.wait_ge(adj0_done, g.count(NC, c + 1))
                act.activation(half(feat, c), acc[c][:, :], ACT.Relu).then_inc(feat1, 1)

            def last_features(g, c):
                act.wait_ge(adj1_done, g.count(NC, c + 1))
                wait_past(act, state_split, g.count(NX, NC - NX))
                act.activation(half(h2, c), acc[c][:, :], ACT.Relu).then_inc(h2_ready, 1)

            def hidden(g, n):
                m = n % 2
                act.wait_ge(hid_ps, g.count(4, n + 1))
                wait_past(act, hid_stats, g.count(4, n - 3))
                wait_past(act, hid_stored[n], g.count(16, 0))
                act.activation(hb[:, n, :], small[m][:, :], ACT.Identity, bias=bn1[:, 0, m:m + 1]).then_inc(hid_set, 1)

            def stage(coming, front, lstm, back):
                for k in range(NS):
                    if lstm is not None:
                        gates(lstm, k)
                    if front is not None:
                        if k == 0:
                            first_features(front, 0)
                            first_features(front, 1)
                            if front.loop is None and front.base == 0:
                                act.wait_ge(wih_in, 16 * (2 * MAX_SKIP - 1))
                                for p in range(MAX_SKIP):
                                    act.activation(wih_hi[:, p, :], wih_stage[p], ACT.Identity).then_inc(w_hi_ready, 1)
                                for p in range(MAX_SKIP - 1):
                                    act.activation(whh_hi[:, p, :], whh_stage[p], ACT.Identity).then_inc(w_hi_ready, 1)
                        if k == 2:
                            second_features(front, 0)
                        if k == 4:
                            second_features(front, 1)
                        if k == 7:
                            last_features(front, 0)
                        if k == 10:
                            last_features(front, 1)
                    if back is not None and k == 8:
                        for n in range(4):
                            hidden(back, n)
            periods(act, stage)

            for b in range(B):
                act.wait_ge(hid_in[b], 16)
                if b == 0:
                    act.wait_ge(bn1_ready, 1)
                for m in range(2):
                    act.activation(hid[:, m, b, :], hid[:, m, b, :], ACT.Relu, scale=bns[:, m:m + 1],
                                   bias=bnt[:, m:m + 1]).then_inc(hid_relu, 1)
            act.wait_ge(bn2_ready, 1)

            def output(g):
                for c in range(NC):
                    wait_past(act, y_t, g.count(NC, c + 1 - NC))
                    act.activation(half(feat, c), z[:, g.index, c * CH:(c + 1) * CH], ACT.Identity, scale=bns[:, 0:1],
                                   bias=bnt[:, 0:1]).then_inc(y_set, 1)
            output(Graph(0))
            with act.Fori(0, B - 1) as i:
                output(Graph(1, i))

        @block.vector
        def _(dve):
            def split(source, hi, lo, hi_set, value, done):
                dve.tensor_copy(hi, source).then_inc(hi_set, 1)
                dve.wait_ge(hi_set, value)
                dve.tensor_tensor(lo, source, hi.bitcast(F32), ALU.subtract).then_inc(done, 1)

            def fence(word):
                dve.memset(fence_word[:, word:word + 1], 0.0)

            def ln_moments_of(g, which):
                if which == 1:
                    dve.wait_ge(x1_ready, g.count(NC, NC))
                wait_past(dve, ln_moments[which], g.count(1, 0))
                fence(4 + 2 * which)
                for n in range(NT):
                    ins = dve.bn_stats(stats[:, which, n, :], xa[:, g.index, n, :])
                ins.then_inc(ln_stats[which], 1)
                dve.wait_ge(ln_stats[which], g.count(1, 1))
                wait_past(dve, ln_done[which], g.count(1, 0))
                fence(5 + 2 * which)
                for n in range(NT):
                    ins = dve.bn_aggr(moments[:, which, n, :], stats[:, which, n, :])
                ins.then_inc(ln_moments[which], 1)

            dve.wait_ge(x_first_in, 16)
            ln_moments_of(Graph(0), 0)
            dve.wait_ge(consts_in, 16 * 15)
            dve.tensor_copy(ident_r[:, :], ident[:, :]).then_inc(consts_made, 1)
            dve.tensor_tensor(bias[:, :], bias_in[:, 0, :], bias_in[:, 1, :], ALU.add).then_inc(consts_made, 1)
            for n in range(NT):
                dve.wait_ge(adj_hi_ready, n + 1)
                dve.tensor_tensor(adj_lo[:, n, :], adj_stage[n], adj_hi[:, n, :].bitcast(F32), ALU.subtract).then_inc(adj_lo_ready, 1)
                dve.tensor_tensor(summed[:, n * P:(n + 1) * P], adj_stage[n][:, n * P:(n + 1) * P], ident[:, :],
                                  ALU.mult).then_inc(deg_step, 1)
            tiles = summed[:, :].rearrange("p (n d) -> p n d", d=P)
            dve.wait_ge(deg_step, NT)
            dve.tensor_reduce(diag[:, :], tiles, AX, ALU.add).then_inc(deg_step, 1)
            dve.wait_ge(deg_step, NT + 1)

            def half(buffer, c):
                return buffer[:, c * CH:(c + 1) * CH]

            def tiles_of(buffer, c):
                return buffer[:, c * TPC:(c + 1) * TPC, :]

            def degrees():
                eye = ident[:, :].unsqueeze(1).broadcast_to([P, TPC, P])
                dve.wait_ge(y_lo_set, NC)
                for c in range(NC):
                    dve.wait_ge(rowsum_ps, c + 1)
                    dve.tensor_tensor(tiles_of(tiles, c), gate_ps[c][:, :].rearrange("p (n d) -> p n d", d=P), eye,
                                      ALU.mult).then_inc(deg_step, 1)
                dve.wait_ge(deg_step, NT + 3)
                dve.tensor_reduce(rowsum[:, :], tiles, AX, ALU.add).then_inc(deg_step, 1)
                dve.wait_ge(deg_step, NT + 4)
                dve.tensor_tensor(deg[:, 0, :], colsum[:, :], rowsum[:, :], ALU.add).then_inc(dinv_step, 1)
                dve.wait_ge(dinv_step, 1)
                dve.tensor_tensor(deg[:, 1, :], deg[:, 0, :], diag[:, :], ALU.subtract).then_inc(dinv_step, 1)
                dve.wait_ge(dinv_step, 2)
                dve.tensor_scalar(deg[:, 2, :], deg[:, 1, :], 1.0, None, ALU.add).then_inc(deg_step, 1)

            def inverse_roots():
                dve.wait_ge(dinv_diag, 1)
                dve.wait_ge(y_lo_set, 2 * NC)
                dve.tensor_tensor(tiles, ident[:, :].unsqueeze(1).broadcast_to([P, NT, P]),
                                  dinv[:, :].unsqueeze(2).broadcast_to([P, NT, P]), ALU.mult).then_inc(dinv_step, 1)

            def inverse_root_row():
                for c in range(NC):
                    dve.wait_ge(dinv_ps, c + 1)
                    dve.tensor_copy(half(dinv_row, c), acc[c][:, :]).then_inc(dinv_ready, 1)

            def cells(g, k):
                st = STEPS[k]
                n = st.windows
                dve.wait_ge(gate_read, g.count(NG, gate_used(k, CELL)))
                if st.zero_state:
                    dve.tensor_tensor(cell[:, 0:n], gate[:, IN, 0:n], gate[:, CELL, 0:n], ALU.mult).then_inc(cell_ready, 1)
                    return
                nth = RECURRENT.index(k - 1) + 1
                dve.tensor_tensor(cand[:, 0:n], gate[:, IN, 0:n], gate[:, CELL, 0:n], ALU.mult).then_inc(cand_ready, 1)
                dve.wait_ge(gate_read, g.count(NG, gate_used(k, FORGET)))
                dve.tensor_tensor(cell[:, 0:n], cell[:, 0:n], gate[:, FORGET, 0:n], ALU.mult).then_inc(forgot, 1)
                dve.wait_ge(cand_ready, g.count(NR, nth))
                dve.wait_ge(forgot, g.count(NR, nth))
                dve.tensor_tensor(cell[:, 0:n], cell[:, 0:n], cand[:, 0:n], ALU.add).then_inc(cell_ready, 1)

            def states(g, k):
                st = STEPS[k]
                n = st.windows
                if k == 0:
                    wait_past(dve, state_t, g.count(NC, 0))
                dve.wait_ge(tanh_ready, g.count(NS, k + 1))
                h = st.columns(state) if st.ends_windows else rec[:, 0:n]
                dve.tensor_tensor(h, gate[:, OUT, 0:n], cell_tanh[:, 0:n], ALU.mult).then_inc(h_ready, 1)
                if k == NS - 1:
                    return
                dve.wait_ge(h_ready, g.count(NS, k + 1))
                if st.ends_windows:
                    nth = NC + RESPLIT.index(k) + 1
                    split(h, st.columns(state_hi), st.columns(state_lo), state_hi_set, g.count(NX, nth), state_split)
                else:
                    split(h, rec_hi[:, 0:n], rec_lo[:, 0:n], rec_hi_set, g.count(NR, RECURRENT.index(k) + 1), rec_split)

            def first_split(g):
                for c in range(NC):
                    dve.wait_ge(h2_ready, g.count(NC, c + 1))
                    split(half(h2, c), half(state_hi, c), half(state_lo, c), state_hi_set, g.count(NX, c + 1), state_split)

            def source(g, which):
                for c in range(NC):
                    n = which * NC + c + 1
                    dve.wait_ge(y_ps, g.count(2 * NC, n))
                    wait_past(dve, y_lo_set, g.count(2 * NC, n - NC))
                    dve.tensor_tensor(half(summed, c).rearrange("p (n d) -> p n d", d=P),
                                      small[c][:, :].rearrange("p (n d) -> p n d", d=P),
                                      bg[:, which, :].unsqueeze(1).broadcast_to([P, TPC, H]), ALU.add).then_inc(y_summed, 1)
                for c in range(NC):
                    n = which * NC + c + 1
                    dve.wait_ge(y_summed, g.count(2 * NC, n))
                    split(half(summed, c).rearrange("p (n d) -> p n d", d=P), tiles_of(y_hi, c), tiles_of(y_lo, c),
                          y_hi_set, g.count(2 * NC, n), y_lo_set)

            def residual(g):
                for c in range(NC):
                    dve.wait_ge(state_t, g.count(NC, c + 1))
                    dve.tensor_tensor(tiles_of(xa[:, g.index], c), acc[c][:, :].rearrange("p (n d) -> p n d", d=P),
                                      tiles_of(xa[:, g.index], c), ALU.add).then_inc(x1_ready, 1)

            def scaled_features(g):
                dve.wait_ge(ln_done[1], g.count(1, 1))
                dve.scalar_tensor_tensor(out=norm[:, :, :], in0=norm[:, :, :], scalar=0.0,
                                         in1=dinv[:, :].unsqueeze(2).broadcast_to([P, NT, D]),
                                         op0=ALU.max, op1=ALU.mult).then_inc(f_scaled, 1)
                dve.wait_ge(f_scaled, g.count(1, 1))
                wait_past(dve, agg_done, g.count(NC, 0))
                split(norm[:, :, :], f_hi[:, :, :], f_lo[:, :, :], f_hi_set, g.count(1, 1), f_lo_set)

            def scaled_aggregate(g, c):
                dve.wait_ge(agg_done, g.count(NC, c + 1))
                wait_past(dve, hid_ps, g.count(4, 0))
                dve.tensor_tensor(half(agg, c), acc[c][:, :], half(dinv_row, c), ALU.mult).then_inc(agg_scaled, 1)

            def hidden_stats(g):
                for n in range(4):
                    c, m = n // 2, n % 2
                    dve.wait_ge(hid_set, g.count(4, n + 1))
                    fence(n)
                    at = g.base * NC + c if g.loop is None else g.loop * NC + (g.base * NC + c)
                    dve.bn_stats(hstats[:, m, at, :], hb[:, n, :]).then_inc(hid_stats, 1)

            def stage(coming, front, lstm, back):
                start = front is not None and front.loop is None and front.base == 0
                for k in range(NS):
                    if lstm is not None:
                        cells(lstm, k)
                        if k == NS - 1 and front is not None:
                            first_split(front)
                        states(lstm, k)
                    elif k == NS - 1 and front is not None:
                        first_split(front)
                    if k == 0 and back is not None:
                        residual(back)
                        ln_moments_of(back, 1)
                    if k == 0 and front is not None and front.loop is None and front.base == 1:
                        inverse_roots()
                        inverse_root_row()
                    if k == 1 and front is not None:
                        source(front, 0)
                        if start:
                            degrees()
                            for p in range(MAX_SKIP):
                                dve.wait_ge(w_hi_ready, p + 1)
                                dve.tensor_tensor(wih_lo[:, p, :], wih_stage[p], wih_hi[:, p, :].bitcast(F32),
                                                  ALU.subtract).then_inc(w_lo_ready, 1)
                            for p in range(MAX_SKIP - 1):
                                dve.wait_ge(w_hi_ready, MAX_SKIP + p + 1)
                                dve.tensor_tensor(whh_lo[:, p, :], whh_stage[p], whh_hi[:, p, :].bitcast(F32),
                                                  ALU.subtract).then_inc(w_lo_ready, 1)
                            dve.wait_ge(w_lo_ready, 2 * MAX_SKIP - 1)
                    if k == 3 and back is not None:
                        scaled_features(back)
                    if k == 5 and front is not None:
                        source(front, 1)
                    if k == 5 and back is not None:
                        scaled_aggregate(back, 0)
                    if k == 6 and back is not None:
                        scaled_aggregate(back, 1)
                    if k == 7 and coming is not None:
                        if start:
                            dve.wait_ge(x_rest_in, 16 * (B - 1))
                        ln_moments_of(coming, 0)
                    if k == 8 and back is not None:
                        hidden_stats(back)
            periods(dve, stage)

            def batchnorm(which, all_stats, weights, ready):
                w = len(all_stats)
                for m in range(w):
                    ins = dve.bn_aggr(bnm[:, m, :], all_stats[m])
                ins.then_inc(bn_own, 1)
                dve.wait_ge(bn_own, 3 * which + 1)
                dve.tensor_scalar(bnv[:, :], bnm[:, :, 1], EPS, None, ALU.add).then_inc(bn_step, 1)
                dve.wait_ge(bn_rstd, which + 1)
                dve.tensor_tensor(bns[:, 0:w], bnr[:, 0:w], weights[:, 1, :], ALU.mult).then_inc(bn_own, 1)
                dve.wait_ge(bn_own, 3 * which + 2)
                dve.tensor_tensor(bnu[:, 0:w], bnm[:, 0:w, 0], bns[:, 0:w], ALU.mult).then_inc(bn_own, 1)
                dve.wait_ge(bn_own, 3 * which + 3)
                dve.tensor_tensor(bnt[:, 0:w], weights[:, 2, :], bnu[:, 0:w], ALU.subtract).then_inc(ready, 1)

            dve.wait_ge(hid_stats, 4 * B)
            batchnorm(0, [hstats[:, m, :, :].rearrange("p n s -> p (n s)") for m in range(2)], bn1, bn1_ready)
            for n in range(B * NC):
                dve.wait_ge(z_ps, n + 1)
                piece = z[:, n // NC, (n % NC) * CH:(n % NC + 1) * CH]
                dve.tensor_scalar(piece, gate_ps[n % 4][:, :], bn2[:, 0, 0:1], None, ALU.add).then_inc(z_set, 1)
                dve.wait_ge(z_set, n + 1)
                dve.bn_stats(zstats[:, n, :], piece).then_inc(z_stats, 1)
            dve.wait_ge(z_stats, B * NC)
            batchnorm(1, [zstats[:, :, :].rearrange("p n s -> p (n s)")], bn2, bn2_ready)

            def output(g):
                for c in range(NC):
                    dve.wait_ge(y_t, g.count(NC, c + 1))
                    dve.tensor_tensor(tiles_of(xa[:, g.index], c), acc[c][:, :].rearrange("p (n d) -> p n d", d=P),
                                      tiles_of(xa[:, g.index], c), ALU.add).then_inc(y_added, 1)
            with dve.Fori(0, B) as i:
                output(Graph(0, i))

        @block.tensor
        def _(pe):
            def product(bank, left, right, first=True, last=True):
                (a_hi, a_lo), (b_hi, b_lo) = left, right
                pe.matmul(bank, a_hi, b_hi, start=first, stop=False)
                pe.matmul(bank, a_hi, b_lo, start=False, stop=False)
                return pe.matmul(bank, a_lo, b_hi, start=False, stop=last)

            def step(g, k):
                st = STEPS[k]
                n = st.windows
                wait_past(pe, state_split, g.count(NX, state_ready(k)))
                for q in st.gates:
                    wait_past(pe, gate_read, g.count(NG, gate_freed(k, q)))
                    at = slice(q * H, (q + 1) * H)
                    last = product(gate_ps[q][:, 0:n], (wih_hi[:, st.p - 1, at], wih_lo[:, st.p - 1, at]),
                                   (st.columns(state_hi), st.columns(state_lo)), last=st.zero_state)
                    if st.zero_state:
                        last.then_inc(gate_done, 1)
                if not st.zero_state:
                    pe.wait_ge(rec_split, g.count(NR, RECURRENT.index(k - 1) + 1))
                    for q in st.gates:
                        at = slice(q * H, (q + 1) * H)
                        product(gate_ps[q][:, 0:n], (whh_hi[:, st.p - 2, at], whh_lo[:, st.p - 2, at]),
                                (rec_hi[:, 0:n], rec_lo[:, 0:n]), first=False).then_inc(gate_done, 1)

            def transposed(banks, c, tile):
                for i in range(TPC):
                    last = pe.transpose(banks[c][:, i * P:(i + 1) * P], tile(c * TPC + i), ident[:, :])
                return last

            def norm_transposed(g):
                pe.wait_ge(ln_done[0], g.count(1, 1))
                for c in range(NC):
                    wait_past(pe, y_summed, g.count(2 * NC, c + 1 - NC))
                    wait_past(pe, hid_set, g.count(4, c + 3 - 12))
                    transposed(small, c, lambda n: norm[:, n, :]).then_inc(norm_t, 1)

            def state_transposed(g):
                pe.wait_ge(h_ready, g.count(NS, NS))
                for c in range(NC):
                    wait_past(pe, h2_ready, at_most(g.count(NC, NC + c + 1), B * NC))
                    wait_past(pe, agg_scaled, g.count(NC, c + 1 - NC))
                    transposed(acc, c, lambda n: state[:, n * P:(n + 1) * P]).then_inc(state_t, 1)

            def linear(g, which):
                for c in range(NC):
                    if which == 0:
                        pe.wait_ge(feat0, g.count(NC, c + 1))
                    else:
                        pe.wait_ge(feat1, g.count(NC, c + 1))
                        pe.wait_ge(y_summed, g.count(2 * NC, c + 1))
                    for i in range(TPC):
                        n = c * TPC + i
                        last = pe.matmul(small[c][:, i * P:(i + 1) * P], feat[:, n * P:(n + 1) * P], wg[:, which, :],
                                         start=True, stop=True)
                    last.then_inc(y_ps, 1)

            def aggregate_hi(c, hi):
                for n in range(NT):
                    pe.matmul(acc[c][:, :], hi[:, n, :], adj_hi[:, n, c * CH:(c + 1) * CH], start=n == 0, stop=False)
                    pe.matmul(acc[c][:, :], hi[:, n, :], adj_lo[:, n, c * CH:(c + 1) * CH], start=False, stop=False)

            def aggregate_lo(c, lo):
                for n in range(NT):
                    last = pe.matmul(acc[c][:, :], lo[:, n, :], adj_hi[:, n, c * CH:(c + 1) * CH], start=False,
                                     stop=n == NT - 1)
                return last

            def convolution_hi(g, which, c):
                pe.wait_ge(y_hi_set, g.count(2 * NC, which * NC + NC))
                if which == 0:
                    wait_past(pe, x1_ready, g.count(NC, c + 1 - 2 * NC))
                    wait_past(pe, h2_ready, g.count(NC, c + 1 - NC))
                else:
                    wait_past(pe, agg_scaled, g.count(NC, c + 1 - 2 * NC))
                    pe.wait_ge(feat1, g.count(NC, c + 1))
                aggregate_hi(c, y_hi)

            def convolution_lo(g, which, c):
                pe.wait_ge(y_lo_set, g.count(2 * NC, which * NC + NC))
                aggregate_lo(c, y_lo).then_inc(adj0_done if which == 0 else adj1_done, 1)

            def normalised_hi(g, c):
                pe.wait_ge(f_hi_set, g.count(1, 1))
                pe.wait_ge(x1_ready, g.count(NC, c + 1))
                wait_past(pe, feat1, at_most(g.count(NC, 2 * NC + c + 1), B * NC))
                aggregate_hi(c, f_hi)
                for i in range(TPC):
                    pe.matmul(acc[c][:, i * P:(i + 1) * P], f_hi[:, c * TPC + i, :], ident_r[:, :], start=False, stop=False)

            def normalised_lo(g, c):
                pe.wait_ge(f_lo_set, g.count(1, 1))
                for i in range(TPC):
                    pe.matmul(acc[c][:, i * P:(i + 1) * P], f_lo[:, c * TPC + i, :], ident_r[:, :], start=False, stop=False)
                aggregate_lo(c, f_lo).then_inc(agg_done, 1)

            def hidden(g):
                for n in range(4):
                    c, m = n // 2, n % 2
                    pe.wait_ge(agg_scaled, g.count(NC, c + 1))
                    wait_past(pe, hid_set, g.count(4, n - 1))
                    wait_past(pe, y_summed, at_most(g.count(2 * NC, 4 * NC + NC + m + 1), 2 * NC * B))
                    pe.matmul(small[m][:, :], w1[:, m * P:(m + 1) * P], agg[:, c * CH:(c + 1) * CH],
                              start=True, stop=True).then_inc(hid_ps, 1)

            def stage(coming, front, lstm, back):
                start = front is not None and front.loop is None and front.base == 0
                for k in range(NS):
                    if lstm is not None:
                        step(lstm, k)
                    if k == 0 and front is not None:
                        norm_transposed(front)
                        if front.loop is None and front.base == 1:
                            pe.wait_ge(dinv_step, 3)
                            for c in range(NC):
                                pe.wait_ge(h2_ready, c + 1)
                                pe.matmul(acc[c][:, :], ones[:, :], summed[:, c * CH:(c + 1) * CH],
                                          start=True, stop=True).then_inc(dinv_ps, 1)
                    if k == 0 and back is not None:
                        state_transposed(back)
                    if k == 1 and front is not None:
                        linear(front, 0)
                        if start:
                            pe.wait_ge(adj_lo_ready, NT)
                            for c in range(NC):
                                for n in range(NT):
                                    pe.matmul(gate_ps[c][:, :], ones_r[:, :], adj_hi[:, n, c * CH:(c + 1) * CH],
                                              start=n == 0, stop=False)
                                    last = pe.matmul(gate_ps[c][:, :], ones_r[:, :], adj_lo[:, n, c * CH:(c + 1) * CH],
                                                     start=False, stop=n == NT - 1)
                                last.then_inc(rowsum_ps, 1)
                    if k == 2 and front is not None:
                        if front.loop is None and front.base == 1:
                            pe.wait_ge(dinv_ready, NC)
                        convolution_hi(front, 0, 0)
                        convolution_lo(front, 0, 0)
                    if k == 3 and front is not None:
                        convolution_hi(front, 0, 1)
                    if k == 4 and front is not None:
                        convolution_lo(front, 0, 1)
                    if k == 4 and back is not None:
                        normalised_hi(back, 0)
                    if k == 5 and front is not None:
                        linear(front, 1)
                        if start:
                            pe.wait_ge(w_lo_ready, 2 * MAX_SKIP - 1)
                            pe.wait_ge(deg_step, NT + 3)
                    if k == 5 and back is not None:
                        normalised_lo(back, 0)
                    if k == 6 and back is not None:
                        normalised_hi(back, 1)
                        normalised_lo(back, 1)
                    if k == 7 and front is not None:
                        convolution_hi(front, 1, 0)
                        convolution_lo(front, 1, 0)
                    if k == 8 and back is not None:
                        hidden(back)
                    if k == 9 and front is not None:
                        convolution_hi(front, 1, 1)
                    if k == 10 and front is not None:
                        convolution_lo(front, 1, 1)
            pe.wait_ge(consts_in, 16 * 15)
            pe.wait_ge(consts_set, 6)
            pe.wait_ge(consts_made, 2)
            periods(pe, stage)

            for n in range(B * NC):
                b, c = n // NC, n % NC
                pe.wait_ge(hid_relu, 2 * b + 2)
                if n >= 4:
                    pe.wait_ge(z_set, n - 3)
                for m in range(2):
                    last = pe.matmul(gate_ps[n % 4][:, :], w2[:, m, :], hid[:, m, b, c * CH:(c + 1) * CH],
                                     start=m == 0, stop=m == 1)
                last.then_inc(z_ps, 1)

            def output(g):
                for c in range(NC):
                    pe.wait_ge(y_set, g.count(NC, c + 1))
                    wait_past(pe, y_added, g.count(NC, c + 1 - NC))
                    transposed(acc, c, lambda n: feat[:, n * P:(n + 1) * P]).then_inc(y_t, 1)
            output(Graph(0))
            with pe.Fori(0, B - 1) as i:
                output(Graph(1, i))


def kernel(x, adj, L0_gnn_Wg0, L0_gnn_bg0, L0_gnn_Wg1, L0_gnn_bg1, L0_gnn_Wih, L0_gnn_Whh, L0_gnn_bih, L0_gnn_bhh,
           L1_gnn_W1, L1_gnn_b1, L1_gnn_g1, L1_gnn_be1, L1_gnn_W2, L1_gnn_b2, L1_gnn_g2, L1_gnn_be2):
    import numpy as np
    import concourse.bacc as bacc
    from concourse.bass_utils import run_bass_kernel_spmd

    def gate_weights(w):
        return w.transpose(2, 0, 1)

    def gate_bias(b):
        return b.reshape(MAX_SKIP * GATES, H).T

    laid = dict(
        x=x, adj_t=adj.T, wg0=L0_gnn_Wg0, wg1=L0_gnn_Wg1, bg0=L0_gnn_bg0[None, :], bg1=L0_gnn_bg1[None, :],
        wih_t=gate_weights(L0_gnn_Wih), whh_t=gate_weights(L0_gnn_Whh), bih_t=gate_bias(L0_gnn_bih),
        bhh_t=gate_bias(L0_gnn_bhh), w1_t=L1_gnn_W1.T, b1_t=L1_gnn_b1.reshape(2, P).T, g1_t=L1_gnn_g1.reshape(2, P).T,
        be1_t=L1_gnn_be1.reshape(2, P).T, w2_t=L1_gnn_W2.T.reshape(2, P, D).transpose(1, 0, 2),
        b2_t=L1_gnn_b2[:, None], g2_t=L1_gnn_g2[:, None], be2_t=L1_gnn_be2[:, None], ident_in=np.eye(P, dtype=np.float32))
    nc = bacc.Bacc("TRN2", target_bir_lowering=False, num_devices=1, dynamic_dma_scratch_size=1024)
    arrays, args = {}, {}
    for name, a in laid.items():
        a = np.ascontiguousarray(a)
        arrays[f"{name}_dram"] = a
        args[name] = nc.dram_tensor(f"{name}_dram", a.shape, mybir.dt.from_np(a.dtype), kind="ExternalInput").ap()
    out = nc.dram_tensor("out_dram", (B, T, D), F32, kind="ExternalOutput").ap()
    program(nc, out=out, **args)
    r = run_bass_kernel_spmd(nc, [arrays], core_ids=[0])
    return r.results[0]["out_dram"]
```

```python
from contextlib import ExitStack

import concourse.bass as bass
from concourse import mybir

ALU = mybir.AluOpType
ACT = mybir.ActivationFunctionType
AX = mybir.AxisListType.X
F32 = mybir.dt.float32
F32R = mybir.dt.float32r

P = 128
B, T, D, H = 8, 1024, 128, 128
F = 256
NT = T // P
CH = 512
NC = T // CH
TPC = CH // P
MAX_SKIP = 4
EPS = 1e-5
GATES = 4
IN, FORGET, CELL, OUT = range(GATES)


class Step:

    def __init__(self, p, s, first_column, windows):
        self.p, self.s, self.first_column, self.windows = p, s, first_column, windows
        self.zero_state = s == 0
        self.ends_windows = s == p - 1
        self.gates = [IN, CELL, OUT] if self.zero_state else [IN, CELL, FORGET, OUT]

    def columns(self, state):
        last = self.first_column + (self.windows - 1) * self.p + 1
        return state[:, self.first_column:last:self.p]


FIRST_CONSTS, CONSTS = 5, 15
EARLY_TILES = 5


def even(n):
    return n + n % 2


STEPS = [Step(1, 0, c * CH, CH) for c in range(NC)]
for _p in range(2, MAX_SKIP + 1):
    STEPS += [Step(_p, _s, _s, even(T // _p)) for _s in range(_p)]
NS = len(STEPS)
TW = max(even(T // p) * p for p in range(1, MAX_SKIP + 1))
GATE_USES = [(k, g) for k, st in enumerate(STEPS) for g in st.gates]
NG = len(GATE_USES)
RECURRENT = [k for k, st in enumerate(STEPS) if not st.ends_windows]
NR = len(RECURRENT)
RESPLIT = [k for k, st in enumerate(STEPS) if st.ends_windows and st.p < MAX_SKIP]
NX = NC + len(RESPLIT)


def gate_used(k, g):
    return GATE_USES.index((k, g)) + 1


def gate_freed(k, g):
    before = [n for n, (j, gg) in enumerate(GATE_USES) if gg == g and j < k]
    last = max(n for n, (_, gg) in enumerate(GATE_USES) if gg == g)
    return before[-1] + 1 if before else last + 1 - NG


def state_ready(k):
    if k < NC:
        return k + 1
    return NC + sum(j < k and STEPS[j].p < STEPS[k].p for j in RESPLIT)


class Graph:

    def __init__(self, base, loop=None):
        self.base, self.loop = base, loop
        self.index = base if loop is None else loop + base

    def count(self, per, n):
        fixed = self.base * per + n
        return fixed if self.loop is None else self.loop * per + fixed


def wait_past(eng, sem, value):
    if isinstance(value, int) and value <= 0:
        return
    eng.wait_ge(sem, value)


def at_most(value, limit):
    return min(value, limit) if isinstance(value, int) else value


def program(nc, x, adj_t, wg0, wg1, bg0, bg1, wih_t, whh_t, bih_t, bhh_t, w1_t, b1_t, g1_t, be1_t,
            w2_t, b2_t, g2_t, be2_t, ident_in, out):
    scratch = nc.dram_tensor("hidden_scratch", [B, 2, P, T], F32, kind="Internal").ap()
    with ExitStack() as ctx:
        def sb(name, shape, dt=F32):
            return ctx.enter_context(nc.sbuf_tensor(name, shape, dt))

        def sem(name):
            return ctx.enter_context(nc.semaphore(name))

        base = nc.sbuf_base
        base = (base + 31) // 32 * 32
        at = [base]

        def place(name, shape, dt=F32):
            n = 4
            for s in shape[1:]:
                n *= s
            t = nc.alloc_sbuf_tensor_at(name, shape, dt, offset=at[0])
            at[0] += (n + 31) // 32 * 32
            return t

        adj_hi = place("adj_hi", [P, NT, T], F32R)
        adj_lo = place("adj_lo", [P, NT, T], F32R)
        hid = nc.alloc_sbuf_tensor_at("hidden", [P, 2, B, T], F32, offset=base)
        z_at = at[0]
        wih_hi = place("wih_hi", [P, MAX_SKIP, GATES * H], F32R)
        wih_lo = place("wih_lo", [P, MAX_SKIP, GATES * H], F32R)
        whh_hi = place("whh_hi", [P, MAX_SKIP - 1, GATES * H], F32R)
        whh_lo = place("whh_lo", [P, MAX_SKIP - 1, GATES * H], F32R)
        state_hi = place("state_hi", [P, TW], F32R)
        state_lo = place("state_lo", [P, TW], F32R)
        assert at[0] - z_at >= B * T * 4
        z = nc.alloc_sbuf_tensor_at("z", [P, B, T], F32, offset=z_at)
        state = place("state", [P, TW])
        rec = place("rec", [P, CH])
        rec_hi = place("rec_hi", [P, CH], F32R)
        rec_lo = place("rec_lo", [P, CH], F32R)
        gate = place("gate", [P, GATES, CH])
        cell = place("cell", [P, CH])
        cand = place("cand", [P, CH])
        cell_tanh = place("cell_tanh", [P, CH])
        xa = place("xa", [P, B, NT, D])
        norm = place("norm", [P, NT, D])
        feat = place("feat", [P, T])
        h2 = place("h2", [P, T])
        summed = place("summed", [P, T])
        y_hi = place("y_hi", [P, NT, H], F32R)
        y_lo = place("y_lo", [P, NT, H], F32R)
        f_hi = place("f_hi", [P, NT, D], F32R)
        f_lo = place("f_lo", [P, NT, D], F32R)
        agg = place("agg", [P, T])
        hb = place("hb", [P, 4, CH])
        dinv_row = place("dinv_row", [P, T])
        ident = place("ident", [P, P])
        ident_r = place("ident_r", [P, P], F32R)
        ones = place("ones", [P, P])
        ones_r = place("ones_r", [P, P], F32R)
        wg = place("wg", [P, 2, H])
        bg = place("bg", [P, 2, H])
        w1 = place("w1", [P, F])
        w2 = place("w2", [P, 2, D])
        bias_in = place("bias_in", [P, 2, MAX_SKIP * GATES])
        bias = place("bias", [P, MAX_SKIP * GATES])
        bn1 = place("bn1", [P, 3, 2])
        bn2 = place("bn2", [P, 3, 1])
        stats = place("stats", [P, 2, NT, 6])
        moments = place("moments", [P, 2, NT, 2])
        veps = place("veps", [P, 2, NT])
        rstd = place("rstd", [P, 2, NT])
        minus_half = place("minus_half", [P, NT])
        eps = place("eps", [P, NT])
        fence_word = place("fence_word", [P, 8])
        colsum = place("colsum", [P, NT])
        rowsum = place("rowsum", [P, NT])
        diag = place("diag", [P, NT])
        deg = place("deg", [P, 3, NT])
        dinv = place("dinv", [P, NT])
        hstats = place("hstats", [P, 2, B * NC, 6])
        zstats = place("zstats", [P, B * NC, 6])
        bnm = place("bnm", [P, 2, 2])
        bnv = place("bnv", [P, 2])
        bnr = place("bnr", [P, 2])
        bns = place("bns", [P, 2])
        bnt = place("bnt", [P, 2])
        bnu = place("bnu", [P, 2])
        assert at[0] <= nc.sbuf_usable_end, (at[0], nc.sbuf_usable_end)
        adj_stage = [xa[:, n + 1, :, :].rearrange("p a b -> p (a b)") for n in range(NT - 1)] + [h2[:, :]]
        diag_blocks = hb[:, 0:NC, :].rearrange("p c (n d) -> p (c n) d", d=P)
        whh_stage = [agg[:, 0:CH], agg[:, CH:T], cand[:, :]]
        wih_stage = [cell_tanh[:, :], cell[:, :], rec[:, :], dinv_row[:, 0:CH]]

        ps = [ctx.enter_context(nc.psum_tensor(f"bank{i}", [P, CH], F32)) for i in range(8)]
        gate_ps = ps[0:4]
        acc = ps[4:6]
        small = ps[6:8]

        def hid_bank(n, front):
            return (small + small if front is None else small + acc)[n]

        turn = [gate_ps[FORGET], acc[1]]
        OUT_SLOTS = 2 * NC
        out_slot = [feat[:, 0:CH], feat[:, CH:T], h2[:, 0:CH], h2[:, CH:T]]
        out_ps = acc + small
        z_pairs = z[:, :, :].rearrange("p (a b) t -> p a (b t)", b=2)
        xa_pairs = xa[:, :, :, :].rearrange("p (a b) (c n) d -> p a (b c) n d", b=2, c=NC)

        adj_in = [sem(f"adj_in{n}") for n in range(NT)]
        first_consts_in = sem("first_consts_in")
        consts_in, x_first_in, x_rest_in, wih_in = sem("consts_in"), sem("x_first_in"), sem("x_rest_in"), sem("wih_in")
        consts_set, consts_made = sem("consts_set"), sem("consts_made")
        adj_hi_ready, adj_lo_ready = sem("adj_hi_ready"), sem("adj_lo_ready")
        w_hi_ready, w_lo_ready = sem("w_hi_ready"), sem("w_lo_ready")
        deg_step, rowsum_ps, dinv_diag, dinv_ps, dinv_ready = (
            sem("deg_step"), sem("rowsum_ps"), sem("dinv_diag"), sem("dinv_ps"), sem("dinv_ready"))
        ln_stats, ln_moments, ln_veps, ln_rstd, ln_centred, ln_done = (
            [sem(f"{name}{which}") for which in range(2)]
            for name in ("ln_stats", "ln_moments", "ln_veps", "ln_rstd", "ln_centred", "ln_done"))
        norm_t, feat0 = sem("norm_t"), sem("feat0")
        y_ps, y_summed, y_hi_set, y_lo_set = sem("y_ps"), sem("y_summed"), sem("y_hi_set"), sem("y_lo_set")
        adj0_done, feat1 = sem("adj0_done"), sem("feat1")
        adj1_done, h2_ready = sem("adj1_done"), sem("h2_ready")
        state_hi_set, state_split = sem("state_hi_set"), sem("state_split")
        gate_done, gate_read = sem("gate_done"), sem("gate_read")
        cand_ready, forgot, cell_ready, tanh_ready, h_ready = (
            sem("cand_ready"), sem("forgot"), sem("cell_ready"), sem("tanh_ready"), sem("h_ready"))
        rec_hi_set, rec_split = sem("rec_hi_set"), sem("rec_split")
        state_t, x1_ready = sem("state_t"), sem("x1_ready")
        f_scaled, f_hi_set, f_lo_set = sem("f_scaled"), sem("f_hi_set"), sem("f_lo_set")
        agg_done, agg_scaled = sem("agg_done"), sem("agg_scaled")
        hid_ps, hid_set, hid_stats = sem("hid_ps"), sem("hid_set"), sem("hid_stats")
        hid_stored = [sem(f"hid_stored{n}") for n in range(4)]
        hid_in = [sem(f"hid_in{b}") for b in range(B)]
        bn_step, bn_rstd, bn_own, dinv_step = sem("bn_step"), sem("bn_rstd"), sem("bn_own"), sem("dinv_step")
        bn1_ready, bn2_ready = sem("bn1_ready"), sem("bn2_ready")
        hid_relu, z_ps, z_set, z_stats = sem("hid_relu"), sem("z_ps"), sem("z_set"), sem("z_stats")
        y_set, y_t, y_added, y_stored = sem("y_set"), sem("y_t"), sem("y_added"), sem("y_stored")

        def periods(eng, body):
            def one(j, loop=None):
                def graph(g, last=B - 1):
                    return Graph(g, loop) if loop is not None or 0 <= g <= last else None
                body(coming=graph(j + 1), front=graph(j), lstm=graph(j - 1), ended=graph(j - 2),
                     back=graph(j - 3, B - 3), late=graph(j - 2) if loop is None and j >= B else None)
            for j in range(4):
                one(j)
            with eng.Fori(0, B - 5) as i:
                one(4, i)
            for j in range(B - 1, B + 2):
                one(j)

        def normalise_head(eng, g, which):
            eng.wait_ge(ln_moments[which], g.count(1, 1))
            eng.tensor_tensor(veps[:, which, :], moments[:, which, :, 1], eps[:, :], ALU.add).then_inc(ln_veps[which], 1)
            if which == 0:
                wait_past(eng, norm_t, g.count(NC, 0))
                wait_past(eng, f_lo_set, g.count(1, -2))
            else:
                wait_past(eng, norm_t, at_most(g.count(NC, 3 * NC), B * NC))
                wait_past(eng, f_lo_set, g.count(1, 0))
            mean = moments[:, which, :, 0].unsqueeze(2).broadcast_to([P, NT, D])
            eng.tensor_tensor(norm[:, :, :], xa[:, g.index, :, :], mean, ALU.subtract).then_inc(ln_centred[which], 1)

        def normalise_tail(eng, g, which):
            eng.wait_ge(ln_rstd[which], g.count(1, 1))
            eng.wait_ge(ln_centred[which], g.count(1, 1))
            scale = rstd[:, which, :].unsqueeze(2).broadcast_to([P, NT, D])
            eng.tensor_tensor(norm[:, :, :], norm[:, :, :], scale, ALU.mult).then_inc(ln_done[which], 1)

        block = ctx.enter_context(nc.Block())

        @block.sync
        def _(sp):
            sp.dma_start(xa[:, 0, :, :], x[0].rearrange("(n p) d -> p n d", p=P)).then_inc(x_first_in, 16)
            for n in range(NT):
                sp.dma_start(adj_stage[n], adj_t[n * P:(n + 1) * P, :]).then_inc(adj_in[n], 16)
            for p in range(MAX_SKIP):
                sp.dma_start(wih_stage[p], wih_t[:, p, :]).then_inc(wih_in, 16)
            for p in range(1, MAX_SKIP):
                sp.dma_start(whh_stage[p - 1], whh_t[:, p, :]).then_inc(wih_in, 16)
            sp.wait_ge(adj_lo_ready, NT)
            sp.wait_ge(deg_step, NT)
            for b in range(1, B):
                sp.dma_start(xa[:, b, :, :], x[b].rearrange("(n p) d -> p n d", p=P)).then_inc(x_rest_in, 16)

            def stage(coming, front, lstm, ended, back, late):
                for g in (back, late):
                    for n in range(4 if g is not None else 0):
                        c, m = n // 2, n % 2
                        sp.wait_ge(hid_set, g.count(4, n + 1))
                        sp.dma_start(scratch[g.index, m, :, c * CH:(c + 1) * CH], hb[:, n, :]).then_inc(hid_stored[n], 16)
            periods(sp, stage)
            sp.wait_ge(agg_done, NC * B)
            for n in range(4):
                sp.wait_ge(hid_stored[n], 16 * B)
            for b in range(B):
                sp.dma_start(hid[:, :, b, :], scratch[b].rearrange("m p t -> p m t")).then_inc(hid_in[b], 16)
            with sp.Fori(0, B) as b:
                for c in range(NC):
                    sp.wait_ge(y_added, b * NC + c + 1)
                    sp.dma_start(out[b, c * CH:(c + 1) * CH, :].rearrange("(n p) d -> p n d", p=P),
                                 xa[:, b, c * TPC:(c + 1) * TPC, :]).then_inc(y_stored, 16)
            sp.wait_ge(y_stored, 16 * NC * B)

        @block.gpsimd
        def _(pool):
            pool.memset(ones[:, :], 1.0).then_inc(consts_set, 1)
            pool.memset(ones_r[:, :].bitcast(F32), 1.0).then_inc(consts_set, 1)
            pool.memset(minus_half[:, :], -0.5).then_inc(consts_set, 1)
            pool.memset(eps[:, :], EPS).then_inc(consts_set, 1)
            pool.memset(state_hi[:, T:TW].bitcast(F32), 0.0).then_inc(consts_set, 1)
            pool.memset(state_lo[:, T:TW].bitcast(F32), 0.0).then_inc(consts_set, 1)
            pool.wait_ge(consts_set, 6)

            def root(g, which):
                pool.wait_ge(ln_veps[which], g.count(1, 1))
                pool.tensor_tensor(rstd[:, which, :], veps[:, which, :], minus_half[:, :], ALU.pow).then_inc(ln_rstd[which], 1)

            def layernorm(g, which):
                normalise_head(pool, g, which)
                root(g, which)
                normalise_tail(pool, g, which)

            root(Graph(0), 0)

            def stage(coming, front, lstm, ended, back, late):
                if front is not None and front.loop is None and front.base == 1:
                    pool.wait_ge(deg_step, NT + 5)
                    pool.tensor_tensor(dinv[:, :], deg[:, 2, :], minus_half[:, :], ALU.pow).then_inc(dinv_diag, 1)
                if ended is not None:
                    if ended.loop is None and ended.base == B - 1:
                        root(ended, 1)
                    else:
                        layernorm(ended, 1)
                if coming is not None:
                    layernorm(coming, 0)
            periods(pool, stage)

            for which in range(2):
                pool.wait_ge(bn_step, which + 1)
                pool.tensor_tensor(bnr[:, :], bnv[:, :], minus_half[:, 0:2], ALU.pow).then_inc(bn_rstd, 1)

        @block.scalar
        def _(act):
            constants = [
                (ident[:, :], ident_in), (wg[:, 0, :], wg0), (wg[:, 1, :], wg1),
                (bg[:, 0, :], bg0.broadcast_to([P, H])), (bg[:, 1, :], bg1.broadcast_to([P, H])),
                (w1[:, :], w1_t), (w2[:, :, :], w2_t), (bias_in[:, 0, :], bih_t), (bias_in[:, 1, :], bhh_t),
                (bn1[:, 0, :], b1_t), (bn1[:, 1, :], g1_t), (bn1[:, 2, :], be1_t),
                (bn2[:, 0, :], b2_t), (bn2[:, 1, :], g2_t), (bn2[:, 2, :], be2_t)]
            for n, (dst, src) in enumerate(constants):
                act.dma_start(dst, src).then_inc(first_consts_in if n < FIRST_CONSTS else consts_in, 16)

            def round_adjacency(tiles):
                for n in tiles:
                    act.wait_ge(adj_in[n], 16)
                    act.activation(adj_hi[:, n, :], adj_stage[n], ACT.Identity,
                                   accum_out=colsum[:, n:n + 1]).then_inc(adj_hi_ready, 1)

            round_adjacency(range(EARLY_TILES))

            def gates(g, k):
                st = STEPS[k]
                n = st.windows
                for q in st.gates:
                    act.wait_ge(gate_done, g.count(NG, gate_used(k, q)))
                    wait_past(act, h_ready if q == OUT else cell_ready, g.count(NS, k))
                    act.activation(gate[:, q, 0:n], gate_ps[q][:, 0:n], ACT.Tanh if q == CELL else ACT.Sigmoid,
                                   bias=bias[:, (st.p - 1) * GATES + q:(st.p - 1) * GATES + q + 1]).then_inc(gate_read, 1)
                act.wait_ge(cell_ready, g.count(NS, k + 1))
                act.activation(cell_tanh[:, 0:n], cell[:, 0:n], ACT.Tanh).then_inc(tanh_ready, 1)

            def half(buffer, c):
                return buffer[:, c * CH:(c + 1) * CH]

            def first_features(g, c):
                act.wait_ge(norm_t, g.count(NC, c + 1))
                wait_past(act, y_ps, g.count(2 * NC, 0))
                act.activation(half(feat, c), small[c][:, :], ACT.Relu).then_inc(feat0, 1)

            def second_features(g, c):
                act.wait_ge(adj0_done, g.count(NC, c + 1))
                act.activation(half(feat, c), acc[c][:, :], ACT.Relu).then_inc(feat1, 1)

            def last_features(g, c):
                act.wait_ge(adj1_done, g.count(NC, c + 1))
                wait_past(act, state_split, g.count(NX, NC - NX))
                act.activation(half(h2, c), acc[c][:, :], ACT.Relu).then_inc(h2_ready, 1)

            def hidden(g, n, front):
                m = n % 2
                act.wait_ge(hid_ps, g.count(4, n + 1))
                wait_past(act, hid_stats, g.count(4, n - 3))
                wait_past(act, hid_stored[n], g.count(16, 0))
                act.activation(hb[:, n, :], hid_bank(n, front)[:, :], ACT.Identity, bias=bn1[:, 0, m:m + 1]).then_inc(hid_set, 1)

            def stage(coming, front, lstm, ended, back, late):
                for k in range(NS):
                    if k == 0 and front is not None:
                        first_features(front, 0)
                        first_features(front, 1)
                    if lstm is not None:
                        gates(lstm, k)
                    if front is not None:
                        if k == 0 and front.loop is None and front.base == 0:
                            round_adjacency(range(EARLY_TILES, NT))
                        if k == 3:
                            if front.loop is None and front.base == 0:
                                act.wait_ge(wih_in, 16 * (2 * MAX_SKIP - 1))
                                for p in range(MAX_SKIP):
                                    act.activation(wih_hi[:, p, :], wih_stage[p], ACT.Identity).then_inc(w_hi_ready, 1)
                                for p in range(MAX_SKIP - 1):
                                    act.activation(whh_hi[:, p, :], whh_stage[p], ACT.Identity).then_inc(w_hi_ready, 1)
                        if k == 4:
                            second_features(front, 0)
                        if k == 5:
                            second_features(front, 1)
                        if k == 8:
                            last_features(front, 0)
                        if k == 10:
                            last_features(front, 1)
                    if back is not None and k in (5, 6):
                        hidden(back, 2 * (k - 5), front)
                        hidden(back, 2 * (k - 5) + 1, front)
                    if late is not None and k == 9:
                        for n in range(4):
                            hidden(late, n, front)
            periods(act, stage)

            for b in range(B):
                act.wait_ge(hid_in[b], 16)
                if b == 0:
                    act.wait_ge(bn1_ready, 1)
                for m in range(2):
                    act.activation(hid[:, m, b, :], hid[:, m, b, :], ACT.Relu, scale=bns[:, m:m + 1],
                                   bias=bnt[:, m:m + 1]).then_inc(hid_relu, 1)
            act.wait_ge(bn2_ready, 1)

            def output(pair):
                for n in range(OUT_SLOTS):
                    wait_past(act, y_t, pair.count(OUT_SLOTS, n + 1 - OUT_SLOTS))
                    act.activation(out_slot[n], z_pairs[:, pair.index, n * CH:(n + 1) * CH], ACT.Identity, scale=bns[:, 0:1],
                                   bias=bnt[:, 0:1]).then_inc(y_set, 1)
            output(Graph(0))
            with act.Fori(0, B // 2 - 1) as i:
                output(Graph(1, i))

        @block.vector
        def _(dve):
            def split(source, hi, lo, hi_set, value, done):
                dve.tensor_copy(hi, source).then_inc(hi_set, 1)
                dve.wait_ge(hi_set, value)
                dve.tensor_tensor(lo, source, hi.bitcast(F32), ALU.subtract).then_inc(done, 1)

            def fence(word):
                dve.memset(fence_word[:, word:word + 1], 0.0)

            def ln_moments_of(g, which):
                if which == 1:
                    dve.wait_ge(x1_ready, g.count(NC, NC))
                wait_past(dve, ln_moments[which], g.count(1, 0))
                fence(4 + 2 * which)
                for n in range(NT):
                    ins = dve.bn_stats(stats[:, which, n, :], xa[:, g.index, n, :])
                ins.then_inc(ln_stats[which], 1)
                dve.wait_ge(ln_stats[which], g.count(1, 1))
                wait_past(dve, ln_done[which], g.count(1, 0))
                fence(5 + 2 * which)
                for n in range(NT):
                    ins = dve.bn_aggr(moments[:, which, n, :], stats[:, which, n, :])
                ins.then_inc(ln_moments[which], 1)

            def split_adjacency(tiles):
                for n in tiles:
                    dve.wait_ge(adj_hi_ready, n + 1)
                    dve.tensor_tensor(adj_lo[:, n, :], adj_stage[n], adj_hi[:, n, :].bitcast(F32), ALU.subtract).then_inc(adj_lo_ready, 1)
                    dve.tensor_tensor(diag_blocks[:, n, :], adj_stage[n][:, n * P:(n + 1) * P], ident[:, :],
                                      ALU.mult).then_inc(deg_step, 1)

            dve.wait_ge(consts_set, 6)
            dve.wait_ge(x_first_in, 16)
            ln_moments_of(Graph(0), 0)
            normalise_head(dve, Graph(0), 0)
            dve.wait_ge(first_consts_in, 16 * FIRST_CONSTS)
            dve.tensor_copy(ident_r[:, :], ident[:, :]).then_inc(consts_made, 1)
            normalise_tail(dve, Graph(0), 0)
            split_adjacency(range(EARLY_TILES))
            tiles = summed[:, :].rearrange("p (n d) -> p n d", d=P)

            def half(buffer, c):
                return buffer[:, c * CH:(c + 1) * CH]

            def tiles_of(buffer, c):
                return buffer[:, c * TPC:(c + 1) * TPC, :]

            def degrees():
                eye = ident[:, :].unsqueeze(1).broadcast_to([P, TPC, P])
                dve.wait_ge(deg_step, NT)
                dve.tensor_reduce(diag[:, :], diag_blocks, AX, ALU.add).then_inc(deg_step, 1)
                dve.wait_ge(deg_step, NT + 1)
                dve.wait_ge(y_lo_set, NC)
                for c in range(NC):
                    dve.wait_ge(rowsum_ps, c + 1)
                    dve.tensor_tensor(tiles_of(tiles, c), gate_ps[c][:, :].rearrange("p (n d) -> p n d", d=P), eye,
                                      ALU.mult).then_inc(deg_step, 1)
                dve.wait_ge(deg_step, NT + 3)
                dve.tensor_reduce(rowsum[:, :], tiles, AX, ALU.add).then_inc(deg_step, 1)
                dve.wait_ge(deg_step, NT + 4)
                dve.tensor_tensor(deg[:, 0, :], colsum[:, :], rowsum[:, :], ALU.add).then_inc(dinv_step, 1)
                dve.wait_ge(dinv_step, 1)
                dve.tensor_tensor(deg[:, 1, :], deg[:, 0, :], diag[:, :], ALU.subtract).then_inc(dinv_step, 1)
                dve.wait_ge(dinv_step, 2)
                dve.tensor_scalar(deg[:, 2, :], deg[:, 1, :], 1.0, None, ALU.add).then_inc(deg_step, 1)

            def inverse_roots():
                dve.wait_ge(dinv_diag, 1)
                dve.wait_ge(y_lo_set, 2 * NC)
                dve.tensor_tensor(tiles, ident[:, :].unsqueeze(1).broadcast_to([P, NT, P]),
                                  dinv[:, :].unsqueeze(2).broadcast_to([P, NT, P]), ALU.mult).then_inc(dinv_step, 1)

            def inverse_root_row():
                for c in range(NC):
                    dve.wait_ge(dinv_ps, c + 1)
                    dve.tensor_copy(half(dinv_row, c), acc[c][:, :]).then_inc(dinv_ready, 1)

            def cells(g, k):
                st = STEPS[k]
                n = st.windows
                dve.wait_ge(gate_read, g.count(NG, gate_used(k, CELL)))
                if st.zero_state:
                    dve.tensor_tensor(cell[:, 0:n], gate[:, IN, 0:n], gate[:, CELL, 0:n], ALU.mult).then_inc(cell_ready, 1)
                    return
                nth = RECURRENT.index(k - 1) + 1
                dve.tensor_tensor(cand[:, 0:n], gate[:, IN, 0:n], gate[:, CELL, 0:n], ALU.mult).then_inc(cand_ready, 1)
                dve.wait_ge(gate_read, g.count(NG, gate_used(k, FORGET)))
                dve.tensor_tensor(cell[:, 0:n], cell[:, 0:n], gate[:, FORGET, 0:n], ALU.mult).then_inc(forgot, 1)
                dve.wait_ge(cand_ready, g.count(NR, nth))
                dve.wait_ge(forgot, g.count(NR, nth))
                dve.tensor_tensor(cell[:, 0:n], cell[:, 0:n], cand[:, 0:n], ALU.add).then_inc(cell_ready, 1)

            def states(g, k):
                st = STEPS[k]
                n = st.windows
                if k == 0:
                    wait_past(dve, state_t, g.count(NC, 0))
                dve.wait_ge(tanh_ready, g.count(NS, k + 1))
                h = st.columns(state) if st.ends_windows else rec[:, 0:n]
                dve.tensor_tensor(h, gate[:, OUT, 0:n], cell_tanh[:, 0:n], ALU.mult).then_inc(h_ready, 1)
                if k == NS - 1:
                    return
                dve.wait_ge(h_ready, g.count(NS, k + 1))
                if st.ends_windows:
                    nth = NC + RESPLIT.index(k) + 1
                    split(h, st.columns(state_hi), st.columns(state_lo), state_hi_set, g.count(NX, nth), state_split)
                else:
                    split(h, rec_hi[:, 0:n], rec_lo[:, 0:n], rec_hi_set, g.count(NR, RECURRENT.index(k) + 1), rec_split)

            def first_split(g):
                for c in range(NC):
                    dve.wait_ge(h2_ready, g.count(NC, c + 1))
                    split(half(h2, c), half(state_hi, c), half(state_lo, c), state_hi_set, g.count(NX, c + 1), state_split)

            def source(g, which):
                for c in range(NC):
                    n = which * NC + c + 1
                    dve.wait_ge(y_ps, g.count(2 * NC, n))
                    wait_past(dve, y_lo_set, g.count(2 * NC, n - NC))
                    dve.tensor_tensor(half(summed, c).rearrange("p (n d) -> p n d", d=P),
                                      small[c][:, :].rearrange("p (n d) -> p n d", d=P),
                                      bg[:, which, :].unsqueeze(1).broadcast_to([P, TPC, H]), ALU.add).then_inc(y_summed, 1)
                for c in range(NC):
                    dve.wait_ge(y_summed, g.count(2 * NC, which * NC + c + 1))
                    wait_past(dve, adj1_done if which == 0 else adj0_done, g.count(NC, 0 if which == 0 else NC))
                    dve.tensor_copy(tiles_of(y_hi, c), half(summed, c).rearrange("p (n d) -> p n d", d=P)).then_inc(y_hi_set, 1)
                for c in range(NC):
                    dve.wait_ge(y_hi_set, g.count(2 * NC, which * NC + c + 1))
                    dve.tensor_tensor(tiles_of(y_lo, c), half(summed, c).rearrange("p (n d) -> p n d", d=P),
                                      tiles_of(y_hi, c).bitcast(F32), ALU.subtract).then_inc(y_lo_set, 1)

            def residual(g):
                for c in range(NC):
                    dve.wait_ge(state_t, g.count(NC, c + 1))
                    dve.tensor_tensor(tiles_of(xa[:, g.index], c), turn[c][:, :].rearrange("p (n d) -> p n d", d=P),
                                      tiles_of(xa[:, g.index], c), ALU.add).then_inc(x1_ready, 1)

            def scaled_features(g):
                dve.wait_ge(ln_done[1], g.count(1, 1))
                dve.scalar_tensor_tensor(out=norm[:, :, :], in0=norm[:, :, :], scalar=0.0,
                                         in1=dinv[:, :].unsqueeze(2).broadcast_to([P, NT, D]),
                                         op0=ALU.max, op1=ALU.mult).then_inc(f_scaled, 1)
                dve.wait_ge(f_scaled, g.count(1, 1))
                wait_past(dve, agg_done, g.count(NC, 0))
                split(norm[:, :, :], f_hi[:, :, :], f_lo[:, :, :], f_hi_set, g.count(1, 1), f_lo_set)

            def scaled_aggregate(g, c):
                dve.wait_ge(agg_done, g.count(NC, c + 1))
                wait_past(dve, hid_ps, g.count(4, 0))
                dve.tensor_tensor(half(agg, c), acc[c][:, :], half(dinv_row, c), ALU.mult).then_inc(agg_scaled, 1)

            def hidden_stats(g):
                for n in range(4):
                    c, m = n // 2, n % 2
                    dve.wait_ge(hid_set, g.count(4, n + 1))
                    fence(n)
                    at = g.base * NC + c if g.loop is None else g.loop * NC + (g.base * NC + c)
                    dve.bn_stats(hstats[:, m, at, :], hb[:, n, :]).then_inc(hid_stats, 1)

            def split_weights():
                dve.wait_ge(consts_in, 16 * (CONSTS - FIRST_CONSTS))
                dve.tensor_tensor(bias[:, :], bias_in[:, 0, :], bias_in[:, 1, :], ALU.add).then_inc(consts_made, 1)
                for n, (lo, stage_, hi) in enumerate(
                        [(wih_lo[:, p, :], wih_stage[p], wih_hi[:, p, :]) for p in range(MAX_SKIP)]
                        + [(whh_lo[:, p, :], whh_stage[p], whh_hi[:, p, :]) for p in range(MAX_SKIP - 1)]):
                    dve.wait_ge(w_hi_ready, n + 1)
                    dve.tensor_tensor(lo, stage_, hi.bitcast(F32), ALU.subtract).then_inc(w_lo_ready, 1)
                dve.wait_ge(w_lo_ready, 2 * MAX_SKIP - 1)

            def stage(coming, front, lstm, ended, back, late):
                start = front is not None and front.loop is None and front.base == 0
                alone = lstm is None and not start
                for k in range(NS):
                    if lstm is not None:
                        cells(lstm, k)
                    if k == NS - 1 and front is not None:
                        first_split(front)
                    if lstm is not None:
                        states(lstm, k)
                    if k == 1 and ended is not None:
                        residual(ended)
                        if alone:
                            ln_moments_of(ended, 1)
                            normalise_head(dve, ended, 1)
                            normalise_tail(dve, ended, 1)
                    if k == 0 and front is not None and front.loop is None and front.base == 1:
                        inverse_roots()
                        inverse_root_row()
                    if k == 1 and front is not None:
                        source(front, 0)
                        if start:
                            split_adjacency(range(EARLY_TILES, NT))
                    if k == 2 and back is not None:
                        scaled_aggregate(back, 0)
                    if k == 2 and ended is not None and not alone:
                        ln_moments_of(ended, 1)
                    if k == 3 and back is not None:
                        scaled_aggregate(back, 1)
                    if k == 4 and start:
                        split_weights()
                        degrees()
                    if k == 5 and ended is not None:
                        scaled_features(ended)
                    if k == 6 and front is not None:
                        source(front, 1)
                    if k == 9 and back is not None:
                        hidden_stats(back)
                    if k == 4 and coming is not None:
                        if start:
                            dve.wait_ge(x_rest_in, 16 * (B - 1))
                        ln_moments_of(coming, 0)
                    if late is not None and k in (7, 8):
                        scaled_aggregate(late, k - 7)
                    if k == 9 and late is not None:
                        hidden_stats(late)
            periods(dve, stage)

            def batchnorm(which, all_stats, weights, ready):
                w = len(all_stats)
                for m in range(w):
                    ins = dve.bn_aggr(bnm[:, m, :], all_stats[m])
                ins.then_inc(bn_own, 1)
                dve.wait_ge(bn_own, 3 * which + 1)
                dve.tensor_scalar(bnv[:, :], bnm[:, :, 1], EPS, None, ALU.add).then_inc(bn_step, 1)
                dve.wait_ge(bn_rstd, which + 1)
                dve.tensor_tensor(bns[:, 0:w], bnr[:, 0:w], weights[:, 1, :], ALU.mult).then_inc(bn_own, 1)
                dve.wait_ge(bn_own, 3 * which + 2)
                dve.tensor_tensor(bnu[:, 0:w], bnm[:, 0:w, 0], bns[:, 0:w], ALU.mult).then_inc(bn_own, 1)
                dve.wait_ge(bn_own, 3 * which + 3)
                dve.tensor_tensor(bnt[:, 0:w], weights[:, 2, :], bnu[:, 0:w], ALU.subtract).then_inc(ready, 1)

            dve.wait_ge(hid_stats, 4 * B)
            batchnorm(0, [hstats[:, m, :, :].rearrange("p n s -> p (n s)") for m in range(2)], bn1, bn1_ready)
            for n in range(B * NC):
                dve.wait_ge(z_ps, n + 1)
                piece = z[:, n // NC, (n % NC) * CH:(n % NC + 1) * CH]
                dve.tensor_scalar(piece, gate_ps[n % 4][:, :], bn2[:, 0, 0:1], None, ALU.add).then_inc(z_set, 1)
                dve.wait_ge(z_set, n + 1)
                dve.bn_stats(zstats[:, n, :], piece).then_inc(z_stats, 1)
            dve.wait_ge(z_stats, B * NC)
            batchnorm(1, [zstats[:, :, :].rearrange("p n s -> p (n s)")], bn2, bn2_ready)

            with dve.Fori(0, B // 2) as i:
                pair = Graph(0, i)
                for n in range(OUT_SLOTS):
                    dve.wait_ge(y_t, pair.count(OUT_SLOTS, n + 1))
                    x1_half = xa_pairs[:, pair.index, n, :, :]
                    dve.tensor_tensor(x1_half, out_ps[n][:, :].rearrange("p (n d) -> p n d", d=P), x1_half,
                                      ALU.add).then_inc(y_added, 1)

        @block.tensor
        def _(pe):
            def product(bank, left, right, first=True, last=True):
                (a_hi, a_lo), (b_hi, b_lo) = left, right
                pe.matmul(bank, a_hi, b_hi, start=first, stop=False)
                pe.matmul(bank, a_hi, b_lo, start=False, stop=False)
                return pe.matmul(bank, a_lo, b_hi, start=False, stop=last)

            def step(g, k):
                st = STEPS[k]
                n = st.windows
                wait_past(pe, state_split, g.count(NX, state_ready(k)))
                for q in st.gates:
                    wait_past(pe, gate_read, g.count(NG, gate_freed(k, q)))
                    if k == NC + 1 and q == FORGET:
                        wait_past(pe, x1_ready, g.count(NC, 1 - NC))
                    at = slice(q * H, (q + 1) * H)
                    last = product(gate_ps[q][:, 0:n], (wih_hi[:, st.p - 1, at], wih_lo[:, st.p - 1, at]),
                                   (st.columns(state_hi), st.columns(state_lo)), last=st.zero_state)
                    if st.zero_state:
                        last.then_inc(gate_done, 1)
                if not st.zero_state:
                    pe.wait_ge(rec_split, g.count(NR, RECURRENT.index(k - 1) + 1))
                    for q in st.gates:
                        at = slice(q * H, (q + 1) * H)
                        product(gate_ps[q][:, 0:n], (whh_hi[:, st.p - 2, at], whh_lo[:, st.p - 2, at]),
                                (rec_hi[:, 0:n], rec_lo[:, 0:n]), first=False).then_inc(gate_done, 1)

            def transposed(banks, c, tile):
                for i in range(TPC):
                    last = pe.transpose(banks[c][:, i * P:(i + 1) * P], tile(c * TPC + i), ident[:, :])
                return last

            def norm_transposed(g):
                pe.wait_ge(ln_done[0], g.count(1, 1))
                for c in range(NC):
                    wait_past(pe, y_summed, g.count(2 * NC, c + 1 - NC))
                    transposed(small, c, lambda n: norm[:, n, :]).then_inc(norm_t, 1)

            def state_transposed(g):
                pe.wait_ge(h_ready, g.count(NS, NS))
                for c in range(NC):
                    if c == 1:
                        wait_past(pe, h2_ready, at_most(g.count(NC, NC + c + 1), B * NC))
                        if g.loop is None and g.base == B - 1:
                            pe.wait_ge(agg_scaled, g.count(NC, c + 1 - NC))
                    transposed(turn, c, lambda n: state[:, n * P:(n + 1) * P]).then_inc(state_t, 1)

            def linear(g, which):
                for c in range(NC):
                    if which == 0:
                        pe.wait_ge(feat0, g.count(NC, c + 1))
                    else:
                        pe.wait_ge(feat1, g.count(NC, c + 1))
                        pe.wait_ge(y_summed, g.count(2 * NC, c + 1))
                        wait_past(pe, hid_set, g.count(4, c + 1 - 3 * 4))
                    for i in range(TPC):
                        n = c * TPC + i
                        last = pe.matmul(small[c][:, i * P:(i + 1) * P], feat[:, n * P:(n + 1) * P], wg[:, which, :],
                                         start=True, stop=True)
                    last.then_inc(y_ps, 1)

            def plus_identity(c, n, part):
                if n // TPC == c:
                    i = n % TPC
                    pe.matmul(acc[c][:, i * P:(i + 1) * P], part[:, n, :], ident_r[:, :], start=False, stop=False)

            def aggregate_hi(c, hi, with_identity=False, arriving=False):
                for n in range(NT):
                    if arriving:
                        pe.wait_ge(adj_lo_ready, n + 1)
                    pe.matmul(acc[c][:, :], hi[:, n, :], adj_hi[:, n, c * CH:(c + 1) * CH], start=n == 0, stop=False)
                    pe.matmul(acc[c][:, :], hi[:, n, :], adj_lo[:, n, c * CH:(c + 1) * CH], start=False, stop=False)
                    if with_identity:
                        plus_identity(c, n, hi)

            def aggregate_lo(c, lo, with_identity=False):
                for n in range(NT):
                    if with_identity:
                        plus_identity(c, n, lo)
                    last = pe.matmul(acc[c][:, :], lo[:, n, :], adj_hi[:, n, c * CH:(c + 1) * CH], start=False,
                                     stop=n == NT - 1)
                return last

            def convolution_hi(g, which, c):
                pe.wait_ge(y_hi_set, g.count(2 * NC, which * NC + NC))
                if which == 0:
                    wait_past(pe, agg_scaled, g.count(NC, c + 1 - 3 * NC))
                    wait_past(pe, h2_ready, g.count(NC, c + 1 - NC))
                    if c == 1:
                        wait_past(pe, x1_ready, g.count(NC, c + 1 - 2 * NC))
                else:
                    pe.wait_ge(feat1, g.count(NC, c + 1))
                    wait_past(pe, hid_set, g.count(4, c + 3 - 3 * 4))
                aggregate_hi(c, y_hi, arriving=which == 0 and g.loop is None and g.base == 0)

            def convolution_lo(g, which, c):
                pe.wait_ge(y_lo_set, g.count(2 * NC, which * NC + NC))
                aggregate_lo(c, y_lo).then_inc(adj0_done if which == 0 else adj1_done, 1)

            def normalised_hi(g, c, ended):
                pe.wait_ge(f_hi_set, g.count(1, 1))
                wait_past(pe, h2_ready, at_most(g.count(NC, 2 * NC + c + 1), B * NC))
                wait_past(pe, agg_scaled, g.count(NC, c + 1 - NC))
                if c == 1:
                    pe.wait_ge(x1_ready, ended.count(NC, c + 1))
                aggregate_hi(c, f_hi, with_identity=True)

            def normalised_lo(g, c):
                pe.wait_ge(f_lo_set, g.count(1, 1))
                aggregate_lo(c, f_lo, with_identity=True).then_inc(agg_done, 1)

            def hidden(g, c, front):
                for m in range(2):
                    pe.wait_ge(agg_scaled, g.count(NC, NC if front is None else c + 1))
                    if front is None:
                        pe.wait_ge(hid_set, g.count(4, 2 * c + m - 1))
                    elif c == 0:
                        wait_past(pe, y_summed, g.count(2 * NC, 6 * NC + m + 1))
                    else:
                        pe.wait_ge(feat1, front.count(NC, m + 1))
                    pe.matmul(hid_bank(2 * c + m, front)[:, :], w1[:, m * P:(m + 1) * P], agg[:, c * CH:(c + 1) * CH],
                              start=True, stop=True).then_inc(hid_ps, 1)

            def row_sums():
                for c in range(NC):
                    for n in range(NT):
                        pe.matmul(gate_ps[c][:, :], ones_r[:, :], adj_hi[:, n, c * CH:(c + 1) * CH],
                                  start=n == 0, stop=False)
                        last = pe.matmul(gate_ps[c][:, :], ones_r[:, :], adj_lo[:, n, c * CH:(c + 1) * CH],
                                         start=False, stop=n == NT - 1)
                    last.then_inc(rowsum_ps, 1)

            def spread_inverse_roots():
                pe.wait_ge(dinv_step, 3)
                for c in range(NC):
                    pe.wait_ge(h2_ready, c + 1)
                    pe.matmul(acc[c][:, :], ones[:, :], summed[:, c * CH:(c + 1) * CH],
                              start=True, stop=True).then_inc(dinv_ps, 1)

            def stage(coming, front, lstm, ended, back, late):
                start = front is not None and front.loop is None and front.base == 0
                second = front is not None and front.loop is None and front.base == 1
                for k in range(NS):
                    if k == 0 and front is not None:
                        norm_transposed(front)
                    if lstm is not None:
                        step(lstm, k)
                    if k == 0 and second:
                        spread_inverse_roots()
                    if k == 0 and ended is not None:
                        state_transposed(ended)
                    if k == 1:
                        if back is not None:
                            normalised_hi(back, 0, ended)
                        if front is not None:
                            linear(front, 0)
                    if k == 2:
                        if back is not None:
                            normalised_lo(back, 0)
                            normalised_hi(back, 1, ended)
                    if k == 3:
                        if back is not None:
                            normalised_lo(back, 1)
                        if second:
                            pe.wait_ge(dinv_ready, NC)
                        if front is not None:
                            convolution_hi(front, 0, 0)
                    if k == 4 and front is not None:
                        convolution_lo(front, 0, 0)
                        convolution_hi(front, 0, 1)
                    if k == 5:
                        if front is not None:
                            convolution_lo(front, 0, 1)
                        if start:
                            row_sums()
                        if back is not None:
                            hidden(back, 0, front)
                    if k == 6 and front is not None:
                        linear(front, 1)
                    if k == 6 and back is not None:
                        hidden(back, 1, front)
                    if k == 7 and front is not None:
                        convolution_hi(front, 1, 0)
                    if k == 8 and front is not None:
                        convolution_lo(front, 1, 0)
                    if k == 9 and front is not None:
                        convolution_hi(front, 1, 1)
                    if k == 10 and front is not None:
                        convolution_lo(front, 1, 1)
                    if late is not None:
                        if k == 6:
                            normalised_hi(late, 0, ended)
                        if k == 7:
                            normalised_lo(late, 0)
                            normalised_hi(late, 1, ended)
                        if k == 8:
                            normalised_lo(late, 1)
                        if k == 9:
                            hidden(late, 0, front)
                            hidden(late, 1, front)
                if start:
                    pe.wait_ge(consts_made, 2)
                    pe.wait_ge(w_lo_ready, 2 * MAX_SKIP - 1)
                    pe.wait_ge(deg_step, NT + 3)
            pe.wait_ge(first_consts_in, 16 * FIRST_CONSTS)
            pe.wait_ge(consts_set, 6)
            periods(pe, stage)

            for n in range(B * NC):
                b, c = n // NC, n % NC
                pe.wait_ge(hid_relu, 2 * b + 2)
                if n >= 4:
                    pe.wait_ge(z_set, n - 3)
                for m in range(2):
                    last = pe.matmul(gate_ps[n % 4][:, :], w2[:, m, :], hid[:, m, b, c * CH:(c + 1) * CH],
                                     start=m == 0, stop=m == 1)
                last.then_inc(z_ps, 1)

            def output(pair):
                for n in range(OUT_SLOTS):
                    pe.wait_ge(y_set, pair.count(OUT_SLOTS, n + 1))
                    wait_past(pe, y_added, pair.count(OUT_SLOTS, n + 1 - OUT_SLOTS))
                    transposed(out_ps, n, lambda i: out_slot[n][:, i % TPC * P:(i % TPC + 1) * P]).then_inc(y_t, 1)
            output(Graph(0))
            with pe.Fori(0, B // 2 - 1) as i:
                output(Graph(1, i))


def kernel(x, adj, L0_gnn_Wg0, L0_gnn_bg0, L0_gnn_Wg1, L0_gnn_bg1, L0_gnn_Wih, L0_gnn_Whh, L0_gnn_bih, L0_gnn_bhh,
           L1_gnn_W1, L1_gnn_b1, L1_gnn_g1, L1_gnn_be1, L1_gnn_W2, L1_gnn_b2, L1_gnn_g2, L1_gnn_be2):
    import numpy as np
    import concourse.bacc as bacc
    from concourse.bass_utils import run_bass_kernel_spmd

    def gate_weights(w):
        return w.transpose(2, 0, 1)

    def gate_bias(b):
        return b.reshape(MAX_SKIP * GATES, H).T

    laid = dict(
        x=x, adj_t=adj.T, wg0=L0_gnn_Wg0, wg1=L0_gnn_Wg1, bg0=L0_gnn_bg0[None, :], bg1=L0_gnn_bg1[None, :],
        wih_t=gate_weights(L0_gnn_Wih), whh_t=gate_weights(L0_gnn_Whh), bih_t=gate_bias(L0_gnn_bih),
        bhh_t=gate_bias(L0_gnn_bhh), w1_t=L1_gnn_W1.T, b1_t=L1_gnn_b1.reshape(2, P).T, g1_t=L1_gnn_g1.reshape(2, P).T,
        be1_t=L1_gnn_be1.reshape(2, P).T, w2_t=L1_gnn_W2.T.reshape(2, P, D).transpose(1, 0, 2),
        b2_t=L1_gnn_b2[:, None], g2_t=L1_gnn_g2[:, None], be2_t=L1_gnn_be2[:, None], ident_in=np.eye(P, dtype=np.float32))
    nc = bacc.Bacc("TRN2", target_bir_lowering=False, num_devices=1, dynamic_dma_scratch_size=1024)
    arrays, args = {}, {}
    for name, a in laid.items():
        a = np.ascontiguousarray(a)
        arrays[f"{name}_dram"] = a
        args[name] = nc.dram_tensor(f"{name}_dram", a.shape, mybir.dt.from_np(a.dtype), kind="ExternalInput").ap()
    out = nc.dram_tensor("out_dram", (B, T, D), F32, kind="ExternalOutput").ap()
    program(nc, out=out, **args)
    r = run_bass_kernel_spmd(nc, [arrays], core_ids=[0])
    return r.results[0]["out_dram"]
```

```python
from contextlib import ExitStack

import concourse.bass as bass
from concourse import mybir

ALU = mybir.AluOpType
ACT = mybir.ActivationFunctionType
AX = mybir.AxisListType.X
F32 = mybir.dt.float32
F32R = mybir.dt.float32r

P = 128
B, T, D, H = 8, 1024, 128, 128
F = 256
NT = T // P
CH = 512
NC = T // CH
TPC = CH // P
MAX_SKIP = 4
EPS = 1e-5
GATES = 4
IN, FORGET, CELL, OUT = range(GATES)


class Step:

    def __init__(self, p, s, first_column, windows):
        self.p, self.s, self.first_column, self.windows = p, s, first_column, windows
        self.zero_state = s == 0
        self.ends_windows = s == p - 1
        self.gates = [IN, CELL, OUT] if self.zero_state else [IN, CELL, FORGET, OUT]

    def columns(self, state):
        last = self.first_column + (self.windows - 1) * self.p + 1
        return state[:, self.first_column:last:self.p]


FIRST_CONSTS, CONSTS = 3, 15
EARLY_TILES = 4


SPILLED = B // 2
W2_ORDER = list(range(B - 1, SPILLED - 1, -1)) + list(range(SPILLED))


def even(n):
    return n + n % 2


ALL_TILES = range(NT)
FIRST_TILES, LAST_TILES = range(TPC), range(TPC, NT)

STEPS = [Step(1, 0, c * CH, CH) for c in range(NC)]
for _p in range(2, MAX_SKIP + 1):
    STEPS += [Step(_p, _s, _s, even(T // _p)) for _s in range(_p)]
NS = len(STEPS)
TW = max(even(T // p) * p for p in range(1, MAX_SKIP + 1))
GATE_USES = [(k, g) for k, st in enumerate(STEPS) for g in st.gates]
NG = len(GATE_USES)
RECURRENT = [k for k, st in enumerate(STEPS) if not st.ends_windows]
NR = len(RECURRENT)
RESPLIT = [k for k, st in enumerate(STEPS) if st.ends_windows and st.p < MAX_SKIP]
NX = NC + len(RESPLIT)


def gate_used(k, g):
    return GATE_USES.index((k, g)) + 1


def gate_freed(k, g):
    before = [n for n, (j, gg) in enumerate(GATE_USES) if gg == g and j < k]
    last = max(n for n, (_, gg) in enumerate(GATE_USES) if gg == g)
    return before[-1] + 1 if before else last + 1 - NG


def state_ready(k):
    if k < NC:
        return k + 1
    return NC + sum(j < k and STEPS[j].p < STEPS[k].p for j in RESPLIT)


class Graph:

    def __init__(self, base, loop=None):
        self.base, self.loop = base, loop
        self.index = base if loop is None else loop + base

    def count(self, per, n):
        fixed = self.base * per + n
        return fixed if self.loop is None else self.loop * per + fixed


def wait_past(eng, sem, value):
    if isinstance(value, int) and value <= 0:
        return
    eng.wait_ge(sem, value)


def at_most(value, limit):
    return min(value, limit) if isinstance(value, int) else value


def program(nc, x, adj_t, wg0, wg1, bg0, bg1, wih_t, whh_t, bih_t, bhh_t, w1_t, b1_t, g1_t, be1_t,
            w2_t, b2_t, g2_t, be2_t, ident_in, out):
    scratch = nc.dram_tensor("hidden_scratch", [SPILLED, 4, P, CH], F32, kind="Internal").ap()
    with ExitStack() as ctx:
        def sem(name):
            return ctx.enter_context(nc.semaphore(name))

        base = nc.sbuf_base
        base = (base + 31) // 32 * 32
        at = [base]

        def place(name, shape, dt=F32):
            n = 4
            for s in shape[1:]:
                n *= s
            t = nc.alloc_sbuf_tensor_at(name, shape, dt, offset=at[0])
            at[0] += (n + 31) // 32 * 32
            return t

        adj_hi = place("adj_hi", [P, NT, T], F32R)
        adj_lo = place("adj_lo", [P, NT, T], F32R)
        hid = nc.alloc_sbuf_tensor_at("hidden", [P, SPILLED, 4, CH], F32, offset=base)
        last_hid = nc.alloc_sbuf_tensor_at("last_hidden", [P, 4, CH], F32, offset=base + NT * T * 4)
        z_at = at[0]
        wih_hi = place("wih_hi", [P, MAX_SKIP, GATES * H], F32R)
        wih_lo = place("wih_lo", [P, MAX_SKIP, GATES * H], F32R)
        whh_hi = place("whh_hi", [P, MAX_SKIP - 1, GATES * H], F32R)
        whh_lo = place("whh_lo", [P, MAX_SKIP - 1, GATES * H], F32R)
        state_hi = place("state_hi", [P, TW], F32R)
        state_lo = place("state_lo", [P, TW], F32R)
        assert at[0] - z_at >= B * T * 4
        z = nc.alloc_sbuf_tensor_at("z", [P, B, T], F32, offset=z_at)
        state = place("state", [P, TW])
        rec = place("rec", [P, CH])
        rec_hi = place("rec_hi", [P, CH], F32R)
        rec_lo = place("rec_lo", [P, CH], F32R)
        gate = place("gate", [P, GATES, CH])
        cell = place("cell", [P, CH])
        cand = place("cand", [P, CH])
        cell_tanh = place("cell_tanh", [P, CH])
        xa = place("xa", [P, B, NT, D])
        norm = place("norm", [P, NT, D])
        hid_over_h2 = nc.alloc_sbuf_tensor_at("hidden_over_h2", [P, 4, CH], F32, offset=at[0])
        feat = place("feat", [P, T])
        h2 = place("h2", [P, T])
        unsplit = place("unsplit", [P, T])
        hid_over_y = nc.alloc_sbuf_tensor_at("hidden_over_y", [P, 4, CH], F32, offset=at[0])
        y_hi = place("y_hi", [P, NT, H], F32R)
        y_lo = place("y_lo", [P, NT, H], F32R)
        f_hi = place("f_hi", [P, NT, D], F32R)
        f_lo = place("f_lo", [P, NT, D], F32R)
        f_t = place("f_t", [P, T])
        spread = nc.alloc_sbuf_tensor_at("spread", [P, T], F32, offset=at[0])
        agg_hi = place("agg_hi", [P, T], F32R)
        whh_first_stage = nc.alloc_sbuf_tensor_at("whh_first_stage", [P, T], F32, offset=at[0])
        agg_lo = place("agg_lo", [P, T], F32R)
        hb = place("hb", [P, 4, CH])
        dinv_row = place("dinv_row", [P, T])
        ident = place("ident", [P, P])
        ones = place("ones", [P, P])
        ones_r = place("ones_r", [P, P], F32R)
        wg = place("wg", [P, 2, H])
        bg = place("bg", [P, 2, H])
        w1_hi = place("w1_hi", [P, F], F32R)
        w1_lo = place("w1_lo", [P, F], F32R)
        w2 = place("w2", [P, 2, D])
        bias_in = place("bias_in", [P, 2, MAX_SKIP * GATES])
        bias = place("bias", [P, MAX_SKIP * GATES])
        bn1 = place("bn1", [P, 3, 2])
        bn2 = place("bn2", [P, 3, 1])
        stats = place("stats", [P, 2, NT, 6])
        moments = place("moments", [P, 2, NT, 2])
        veps = place("veps", [P, 2, NT])
        rstd = place("rstd", [P, 2, NT])
        scale = place("scale", [P, NT])
        minus_half = place("minus_half", [P, NT])
        eps = place("eps", [P, NT])
        fence_word = place("fence_word", [P, 8])
        colsum = place("colsum", [P, NT])
        rowsum = place("rowsum", [P, NT])
        diag = place("diag", [P, NT])
        deg = place("deg", [P, 3, NT])
        dinv = place("dinv", [P, NT])
        hstats = place("hstats", [P, 2, B * NC, 6])
        zstats = place("zstats", [P, B * NC, 6])
        bnm = place("bnm", [P, 2, 2])
        bnv = place("bnv", [P, 2])
        bnr = place("bnr", [P, 2])
        bns = place("bns", [P, 2])
        bnt = place("bnt", [P, 2])
        bnu = place("bnu", [P, 2])
        assert at[0] <= nc.sbuf_usable_end, (at[0], nc.sbuf_usable_end)
        kept_hidden = {B - 4: hb, B - 3: hid_over_h2, B - 2: hid_over_y, B - 1: last_hid}
        adj_stage = [xa[:, n + 1, :, :].rearrange("p a b -> p (a b)") for n in range(NT - 1)] + [h2[:, :]]
        diag_blocks = hb[:, 0:NC, :].rearrange("p c (n d) -> p (c n) d", d=P)
        w1_stage = hb[:, 3, 0:F]
        whh_stage = [whh_first_stage[:, 0:CH], whh_first_stage[:, CH:T], cand[:, :]]
        wih_stage = [cell_tanh[:, :], cell[:, :], rec[:, :], dinv_row[:, 0:CH]]

        ps = [ctx.enter_context(nc.psum_tensor(f"bank{i}", [P, CH], F32)) for i in range(8)]
        gate_ps = ps[0:4]
        acc = ps[4:6]
        small = ps[6:8]

        def hid_bank(n, front):
            return (small + small if front is None else acc + [small[0], gate_ps[FORGET]])[n]


        def is_last(g):
            return g.loop is None and g.base == B - 1

        def agg_bank(g, c):
            return [gate_ps[CELL], gate_ps[OUT]][c] if g.loop is None and g.base == B - 1 else acc[c]

        def turn(g):
            return [gate_ps[FORGET], gate_ps[IN] if g.loop is None and g.base == B - 1 else acc[1]]

        OUT_SLOTS = 2 * NC
        out_slot = [feat[:, 0:CH], feat[:, CH:T], h2[:, 0:CH], h2[:, CH:T]]
        out_ps = acc + small
        z_pairs = z[:, :, :].rearrange("p (a b) t -> p a (b t)", b=2)
        xa_pairs = xa[:, :, :, :].rearrange("p (a b) (c n) d -> p a (b c) n d", b=2, c=NC)

        adj_in = [sem(f"adj_in{n}") for n in range(NT)]
        first_consts_in = sem("first_consts_in")
        consts_in, wih_in = sem("consts_in"), sem("wih_in")
        x_first_in = [sem(f"x_first_in{c}") for c in range(NC)]
        x_second_in, x_rest_in = sem("x_second_in"), sem("x_rest_in")
        consts_set, consts_made = sem("consts_set"), sem("consts_made")
        adj_hi_ready, adj_lo_ready = sem("adj_hi_ready"), sem("adj_lo_ready")
        w_hi_ready, w_lo_ready = sem("w_hi_ready"), sem("w_lo_ready")
        deg_step, rowsum_ps, dinv_diag, dinv_ps, dinv_ready = (
            sem("deg_step"), sem("rowsum_ps"), sem("dinv_diag"), sem("dinv_ps"), sem("dinv_ready"))
        ln_stats, ln_moments, ln_veps, ln_rstd, ln_centred = (
            [sem(f"{name}{which}") for which in range(2)]
            for name in ("ln_stats", "ln_moments", "ln_veps", "ln_rstd", "ln_centred"))
        ln_done = sem("ln_done")
        w1_hi_set, w1_split = sem("w1_hi_set"), sem("w1_split")
        ln_scaled, norm_t, feat0 = sem("ln_scaled"), sem("norm_t"), sem("feat0")
        y_ps, y_summed, y_hi_set, y_lo_set = sem("y_ps"), sem("y_summed"), sem("y_hi_set"), sem("y_lo_set")
        adj0_done, feat1 = sem("adj0_done"), sem("feat1")
        adj1_done, h2_ready = sem("adj1_done"), sem("h2_ready")
        state_hi_set, state_split = sem("state_hi_set"), sem("state_split")
        gate_done, gate_read = sem("gate_done"), sem("gate_read")
        cand_ready, forgot, cell_ready, tanh_ready, h_ready = (
            sem("cand_ready"), sem("forgot"), sem("cell_ready"), sem("tanh_ready"), sem("h_ready"))
        rec_hi_set, rec_split = sem("rec_hi_set"), sem("rec_split")
        state_t, x1_ready = sem("state_t"), sem("x1_ready")
        f_scaled, f_hi_set, f_lo_set = sem("f_scaled"), sem("f_hi_set"), sem("f_lo_set")
        f_t_ps, f_t_set, agg_summed = sem("f_t_ps"), sem("f_t_set"), sem("agg_summed")
        agg_done, agg_scaled, agg_hi_set, agg_split = sem("agg_done"), sem("agg_scaled"), sem("agg_hi_set"), sem("agg_split")
        hid_ps, hid_set, hid_stats = sem("hid_ps"), sem("hid_set"), sem("hid_stats")
        hid_stored = [sem(f"hid_stored{n}") for n in range(4)]
        hid_in = [sem(f"hid_in{b}") for b in range(SPILLED)]
        bn_step, bn_rstd, bn_own, dinv_step = sem("bn_step"), sem("bn_rstd"), sem("bn_own"), sem("dinv_step")
        bn1_ready, bn2_ready = sem("bn1_ready"), sem("bn2_ready")
        hid_relu, z_ps, z_set, z_stats = sem("hid_relu"), sem("z_ps"), sem("z_set"), sem("z_stats")
        y_set, y_t, y_added, y_stored = sem("y_set"), sem("y_t"), sem("y_added"), sem("y_stored")

        def hidden_layer(b):
            layer = hid[:, b, :, :] if b < SPILLED else kept_hidden[b][:, :, :]
            return layer.rearrange("p (c m) t -> p c m t", m=2)

        def hidden_piece(g, n):
            return (hb if g.loop is not None or g.base < SPILLED else kept_hidden[g.base])[:, n, :]

        def periods(eng, body):
            def one(j, loop=None):
                def graph(g, last=B - 1):
                    return Graph(g, loop) if loop is not None or 0 <= g <= last else None
                body(coming=graph(j + 1), front=graph(j), lstm=graph(j - 1), ended=graph(j - 2),
                     back=graph(j - 3, B - 3), late=Graph(B - 2) if loop is None and j >= B else None)
            for j in range(4):
                one(j)
            with eng.Fori(0, B - 5) as i:
                one(4, i)
            for j in range(B - 1, B + 2):
                one(j)

        def normalise_head(eng, g, which):
            eng.wait_ge(ln_moments[which], g.count(1, 1))
            eng.tensor_tensor(veps[:, which, :], moments[:, which, :, 1], eps[:, :], ALU.add).then_inc(ln_veps[which], 1)
            wait_past(eng, f_t_ps, g.count(NC, -2 * NC if which == 0 else 0))
            if which == 0:
                wait_past(eng, norm_t, g.count(NC, 0))
                wait_past(eng, f_lo_set, g.count(1, -2))
            else:
                wait_past(eng, norm_t, at_most(g.count(NC, 3 * NC), B * NC))
                wait_past(eng, f_lo_set, g.count(1, 0))
            mean = moments[:, which, :, 0].unsqueeze(2).broadcast_to([P, NT, D])
            eng.tensor_tensor(norm[:, :, :], xa[:, g.index, :, :], mean, ALU.subtract).then_inc(ln_centred[which], 1)

        def normalise_tail(eng, g):
            eng.wait_ge(ln_rstd[0], g.count(1, 1))
            eng.wait_ge(ln_centred[0], g.count(1, 1))
            scale = rstd[:, 0, :].unsqueeze(2).broadcast_to([P, NT, D])
            eng.tensor_tensor(norm[:, :, :], norm[:, :, :], scale, ALU.mult).then_inc(ln_done, 1)

        block = ctx.enter_context(nc.Block())

        @block.sync
        def _(sp):
            for c in range(NC):
                sp.dma_start(xa[:, 0, c * TPC:(c + 1) * TPC, :],
                             x[0, c * CH:(c + 1) * CH, :].rearrange("(n p) d -> p n d", p=P)).then_inc(x_first_in[c], 16)
            for n in range(NT):
                sp.dma_start(adj_stage[n], adj_t[n * P:(n + 1) * P, :]).then_inc(adj_in[n], 16)
            for p in range(MAX_SKIP):
                sp.dma_start(wih_stage[p], wih_t[:, p, :]).then_inc(wih_in, 16)
            for p in range(1, MAX_SKIP):
                sp.dma_start(whh_stage[p - 1], whh_t[:, p, :]).then_inc(wih_in, 16)
            sp.wait_ge(adj_lo_ready, NT)
            sp.wait_ge(deg_step, NT)
            for b in range(1, B):
                sp.dma_start(xa[:, b, :, :],
                             x[b].rearrange("(n p) d -> p n d", p=P)).then_inc(x_second_in if b == 1 else x_rest_in, 16)

            def stage(coming, front, lstm, ended, back, late):
                if back is not None and (back.loop is not None or back.base < SPILLED):
                    for n in range(4):
                        sp.wait_ge(hid_set, back.count(4, n + 1))
                        sp.dma_start(scratch[back.index, n, :, :], hb[:, n, :]).then_inc(hid_stored[n], 16)
            periods(sp, stage)
            sp.wait_ge(agg_done, NC * B)
            for n in range(4):
                sp.wait_ge(hid_stored[n], 16 * SPILLED)
            for b in range(SPILLED):
                sp.dma_start(hid[:, b, :, :], scratch[b].rearrange("n p t -> p n t")).then_inc(hid_in[b], 16)
            with sp.Fori(0, B) as b:
                for c in range(NC):
                    sp.wait_ge(y_added, b * NC + c + 1)
                    sp.dma_start(out[b, c * CH:(c + 1) * CH, :].rearrange("(n p) d -> p n d", p=P),
                                 xa[:, b, c * TPC:(c + 1) * TPC, :]).then_inc(y_stored, 16)
            sp.wait_ge(y_stored, 16 * NC * B)

        @block.gpsimd
        def _(pool):
            pool.memset(ones[:, :], 1.0).then_inc(consts_set, 1)
            pool.memset(ones_r[:, :].bitcast(F32), 1.0).then_inc(consts_set, 1)
            pool.memset(minus_half[:, :], -0.5).then_inc(consts_set, 1)
            pool.memset(eps[:, :], EPS).then_inc(consts_set, 1)
            pool.memset(state_hi[:, T:TW].bitcast(F32), 0.0).then_inc(consts_set, 1)
            pool.memset(state_lo[:, T:TW].bitcast(F32), 0.0).then_inc(consts_set, 1)
            pool.wait_ge(consts_set, 6)

            def root(g, which):
                pool.wait_ge(ln_veps[which], g.count(1, 1))
                pool.tensor_tensor(rstd[:, which, :], veps[:, which, :], minus_half[:, :], ALU.pow).then_inc(ln_rstd[which], 1)

            def layernorm(g, which):
                normalise_head(pool, g, which)
                root(g, which)
                if which == 0:
                    normalise_tail(pool, g)

            root(Graph(0), 0)

            def stage(coming, front, lstm, ended, back, late):
                if front is not None and front.loop is None and front.base == 1:
                    pool.wait_ge(deg_step, NT + 5)
                    pool.tensor_tensor(dinv[:, :], deg[:, 2, :], minus_half[:, :], ALU.pow).then_inc(dinv_diag, 1)
                if ended is not None:
                    if ended.loop is None and ended.base == B - 1:
                        for c in range(NC):
                            pool.wait_ge(ln_veps[1], ended.count(1, c + 1))
                            pool.tensor_tensor(rstd[:, 1, c * TPC:(c + 1) * TPC], veps[:, 1, c * TPC:(c + 1) * TPC],
                                               minus_half[:, 0:TPC], ALU.pow).then_inc(ln_rstd[1], 1)
                    else:
                        layernorm(ended, 1)
                if coming is not None:
                    layernorm(coming, 0)
            periods(pool, stage)

            for which in range(2):
                pool.wait_ge(bn_step, which + 1)
                pool.tensor_tensor(bnr[:, :], bnv[:, :], minus_half[:, 0:2], ALU.pow).then_inc(bn_rstd, 1)

        @block.scalar
        def _(act):
            constants = [
                (ident[:, :], ident_in), (wg[:, 0, :], wg0), (bg[:, 0, :], bg0.broadcast_to([P, H])),
                (wg[:, 1, :], wg1), (bg[:, 1, :], bg1.broadcast_to([P, H])),
                (w1_stage, w1_t), (w2[:, :, :], w2_t), (bias_in[:, 0, :], bih_t), (bias_in[:, 1, :], bhh_t),
                (bn1[:, 0, :], b1_t), (bn1[:, 1, :], g1_t), (bn1[:, 2, :], be1_t),
                (bn2[:, 0, :], b2_t), (bn2[:, 1, :], g2_t), (bn2[:, 2, :], be2_t)]
            for dst, src in constants[:FIRST_CONSTS]:
                act.dma_start(dst, src).then_inc(first_consts_in, 16)

            def round_adjacency(tiles):
                for n in tiles:
                    act.wait_ge(adj_in[n], 16)
                    act.activation(adj_hi[:, n, :], adj_stage[n], ACT.Identity,
                                   accum_out=colsum[:, n:n + 1]).then_inc(adj_hi_ready, 1)

            round_adjacency(range(EARLY_TILES))

            def gates(g, k):
                st = STEPS[k]
                n = st.windows
                for q in st.gates:
                    act.wait_ge(gate_done, g.count(NG, gate_used(k, q)))
                    wait_past(act, h_ready if q == OUT else cell_ready, g.count(NS, k))
                    act.activation(gate[:, q, 0:n], gate_ps[q][:, 0:n], ACT.Tanh if q == CELL else ACT.Sigmoid,
                                   bias=bias[:, (st.p - 1) * GATES + q:(st.p - 1) * GATES + q + 1]).then_inc(gate_read, 1)
                act.wait_ge(cell_ready, g.count(NS, k + 1))
                act.activation(cell_tanh[:, 0:n], cell[:, 0:n], ACT.Tanh).then_inc(tanh_ready, 1)

            def half(buffer, c):
                return buffer[:, c * CH:(c + 1) * CH]

            def first_features(g, c):
                act.wait_ge(norm_t, g.count(NC, c + 1))
                wait_past(act, y_ps, g.count(2 * NC, 0))
                act.activation(half(feat, c), small[c][:, :], ACT.Relu).then_inc(feat0, 1)

            def second_features(g, c):
                act.wait_ge(adj0_done, g.count(NC, c + 1))
                act.activation(half(feat, c), acc[c][:, :], ACT.Relu).then_inc(feat1, 1)

            def turned_features(g, c):
                act.wait_ge(f_t_ps, g.count(NC, c + 1))
                wait_past(act, agg_summed, g.count(NC, c + 1 - NC))
                bank = turn(g)[c] if is_last(g) else small[c]
                act.activation(half(f_t, c), bank[:, :], ACT.Identity).then_inc(f_t_set, 1)

            def last_features(g, c):
                act.wait_ge(adj1_done, g.count(NC, c + 1))
                wait_past(act, state_split, g.count(NX, NC - NX))
                act.activation(half(h2, c), acc[c][:, :], ACT.Relu).then_inc(h2_ready, 1)

            def hidden(g, n, front):
                m = n % 2
                act.wait_ge(hid_ps, g.count(4, n + 1))
                if g.loop is not None or g.base <= SPILLED:
                    wait_past(act, hid_stats, g.count(4, n - 3))
                    wait_past(act, hid_stored[n], g.count(16, 0))
                act.activation(hidden_piece(g, n), hid_bank(n, front)[:, :], ACT.Identity,
                               bias=bn1[:, 0, m:m + 1]).then_inc(hid_set, 1)

            def stage(coming, front, lstm, ended, back, late):
                for k in range(NS):
                    if k == 0 and front is not None:
                        first_features(front, 0)
                        first_features(front, 1)
                    if lstm is not None:
                        gates(lstm, k)
                    if front is not None:
                        if k == 0 and front.loop is None and front.base == 0:
                            round_adjacency(range(EARLY_TILES, NT))
                            for dst, src in constants[FIRST_CONSTS:]:
                                act.dma_start(dst, src).then_inc(consts_in, 16)
                        if k == 3:
                            if front.loop is None and front.base == 0:
                                act.wait_ge(wih_in, 16 * (2 * MAX_SKIP - 1))
                                for p in range(MAX_SKIP):
                                    act.activation(wih_hi[:, p, :], wih_stage[p], ACT.Identity).then_inc(w_hi_ready, 1)
                                for p in range(MAX_SKIP - 1):
                                    act.activation(whh_hi[:, p, :], whh_stage[p], ACT.Identity).then_inc(w_hi_ready, 1)
                        if k == 4:
                            second_features(front, 0)
                        if k == 5:
                            if ended is not None:
                                turned_features(ended, 0)
                                turned_features(ended, 1)
                            if back is not None:
                                second_features(front, 1)
                        if k == 6 and back is None:
                            second_features(front, 1)
                        if k == 8:
                            last_features(front, 0)
                        if k == 10:
                            last_features(front, 1)
                    if back is not None and k in ((5, 6) if front is None else (6, 7)):
                        first = 2 * (k - (5 if front is None else 6))
                        hidden(back, first, front)
                        hidden(back, first + 1, front)
                    if front is None and lstm is not None and k == 7:
                        turned_features(ended, 0)
                        turned_features(ended, 1)
                if ended is not None and lstm is None:
                    hidden(late, 0, front)
                    hidden(late, 1, front)
                    turned_features(ended, 0)
                    turned_features(ended, 1)
                    hidden(late, 2, front)
                    hidden(late, 3, front)
                    for n in range(4):
                        hidden(ended, n, front)
            periods(act, stage)

            act.wait_ge(bn1_ready, 1)
            act.wait_ge(hid_set, 4 * B)
            for b in W2_ORDER:
                if b < SPILLED:
                    act.wait_ge(hid_in[b], 16)
                for c in range(NC) if b == B - 1 else [slice(0, NC)]:
                    for m in range(2):
                        piece = hidden_layer(b)[:, c, m, :]
                        act.activation(piece, piece, ACT.Relu, scale=bns[:, m:m + 1],
                                       bias=bnt[:, m:m + 1]).then_inc(hid_relu, 1)
            act.wait_ge(bn2_ready, 1)

            def output(pair):
                for n in range(OUT_SLOTS):
                    wait_past(act, y_t, pair.count(OUT_SLOTS, n + 1 - OUT_SLOTS))
                    act.activation(out_slot[n], z_pairs[:, pair.index, n * CH:(n + 1) * CH], ACT.Identity, scale=bns[:, 0:1],
                                   bias=bnt[:, 0:1]).then_inc(y_set, 1)
            output(Graph(0))
            with act.Fori(0, B // 2 - 1) as i:
                output(Graph(1, i))

        @block.vector
        def _(dve):
            def split(source, hi, lo, hi_set, value, done):
                dve.tensor_copy(hi, source).then_inc(hi_set, 1)
                dve.wait_ge(hi_set, value)
                dve.tensor_tensor(lo, source, hi.bitcast(F32), ALU.subtract).then_inc(done, 1)

            def fence(word):
                dve.memset(fence_word[:, word:word + 1], 0.0)

            def ln_moments_of(g, which, arriving=None):
                if which == 1:
                    dve.wait_ge(x1_ready, g.count(NC, NC))
                wait_past(dve, ln_moments[which], g.count(1, 0))
                fence(4 + 2 * which)
                for n in range(NT):
                    if arriving is not None and n % TPC == 0:
                        dve.wait_ge(arriving[n // TPC], 16)
                    ins = dve.bn_stats(stats[:, which, n, :], xa[:, g.index, n, :])
                ins.then_inc(ln_stats[which], 1)
                dve.wait_ge(ln_stats[which], g.count(1, 1))
                wait_past(dve, ln_centred[which], g.count(1, 0))
                fence(5 + 2 * which)
                for n in range(NT):
                    ins = dve.bn_aggr(moments[:, which, n, :], stats[:, which, n, :])
                ins.then_inc(ln_moments[which], 1)

            def split_adjacency(tiles):
                for n in tiles:
                    dve.wait_ge(adj_hi_ready, n + 1)
                    dve.tensor_tensor(adj_lo[:, n, :], adj_stage[n], adj_hi[:, n, :].bitcast(F32), ALU.subtract).then_inc(adj_lo_ready, 1)

            dve.wait_ge(consts_set, 6)
            ln_moments_of(Graph(0), 0, arriving=x_first_in)
            normalise_head(dve, Graph(0), 0)
            normalise_tail(dve, Graph(0))
            split_adjacency(range(EARLY_TILES))
            tiles = spread[:, :].rearrange("p (n d) -> p n d", d=P)

            def half(buffer, c):
                return buffer[:, c * CH:(c + 1) * CH]

            def tiles_of(buffer, c):
                return buffer[:, c * TPC:(c + 1) * TPC, :]

            def diagonal():
                dve.wait_ge(first_consts_in, 16 * FIRST_CONSTS)
                for n in range(NT):
                    dve.tensor_tensor(diag_blocks[:, n, :], adj_stage[n][:, n * P:(n + 1) * P], ident[:, :],
                                      ALU.mult).then_inc(deg_step, 1)
                dve.wait_ge(deg_step, NT)
                dve.tensor_reduce(diag[:, :], diag_blocks, AX, ALU.add).then_inc(deg_step, 1)

            def masked_row_sums(c):
                eye = ident[:, :].unsqueeze(1).broadcast_to([P, TPC, P])
                dve.wait_ge(rowsum_ps, c + 1)
                dve.tensor_tensor(tiles_of(tiles, c), acc[c][:, :].rearrange("p (n d) -> p n d", d=P), eye,
                                  ALU.mult).then_inc(deg_step, 1)

            def degrees():
                dve.wait_ge(deg_step, NT + 3)
                dve.tensor_reduce(rowsum[:, :], tiles, AX, ALU.add).then_inc(deg_step, 1)
                dve.wait_ge(deg_step, NT + 4)
                dve.tensor_tensor(deg[:, 0, :], colsum[:, :], rowsum[:, :], ALU.add).then_inc(dinv_step, 1)
                dve.wait_ge(dinv_step, 1)
                dve.tensor_tensor(deg[:, 1, :], deg[:, 0, :], diag[:, :], ALU.subtract).then_inc(dinv_step, 1)
                dve.wait_ge(dinv_step, 2)
                dve.tensor_scalar(deg[:, 2, :], deg[:, 1, :], 1.0, None, ALU.add).then_inc(deg_step, 1)

            def inverse_roots():
                dve.wait_ge(dinv_diag, 1)
                dve.wait_ge(deg_step, NT + 5)
                dve.tensor_tensor(tiles, ident[:, :].unsqueeze(1).broadcast_to([P, NT, P]),
                                  dinv[:, :].unsqueeze(2).broadcast_to([P, NT, P]), ALU.mult).then_inc(dinv_step, 1)

            def inverse_root_row():
                for c in range(NC):
                    dve.wait_ge(dinv_ps, c + 1)
                    dve.tensor_copy(half(dinv_row, c), acc[c][:, :]).then_inc(dinv_ready, 1)

            def cells(g, k):
                st = STEPS[k]
                n = st.windows
                dve.wait_ge(gate_read, g.count(NG, gate_used(k, CELL)))
                if st.zero_state:
                    dve.tensor_tensor(cell[:, 0:n], gate[:, IN, 0:n], gate[:, CELL, 0:n], ALU.mult).then_inc(cell_ready, 1)
                    return
                nth = RECURRENT.index(k - 1) + 1
                dve.tensor_tensor(cand[:, 0:n], gate[:, IN, 0:n], gate[:, CELL, 0:n], ALU.mult).then_inc(cand_ready, 1)
                dve.wait_ge(gate_read, g.count(NG, gate_used(k, FORGET)))
                dve.tensor_tensor(cell[:, 0:n], cell[:, 0:n], gate[:, FORGET, 0:n], ALU.mult).then_inc(forgot, 1)
                dve.wait_ge(cand_ready, g.count(NR, nth))
                dve.wait_ge(forgot, g.count(NR, nth))
                dve.tensor_tensor(cell[:, 0:n], cell[:, 0:n], cand[:, 0:n], ALU.add).then_inc(cell_ready, 1)

            def states(g, k):
                st = STEPS[k]
                n = st.windows
                if k == 0:
                    wait_past(dve, state_t, g.count(NC, 0))
                dve.wait_ge(tanh_ready, g.count(NS, k + 1))
                h = st.columns(state) if st.ends_windows else rec[:, 0:n]
                dve.tensor_tensor(h, gate[:, OUT, 0:n], cell_tanh[:, 0:n], ALU.mult).then_inc(h_ready, 1)
                if k == NS - 1:
                    return
                dve.wait_ge(h_ready, g.count(NS, k + 1))
                if st.ends_windows:
                    nth = NC + RESPLIT.index(k) + 1
                    split(h, st.columns(state_hi), st.columns(state_lo), state_hi_set, g.count(NX, nth), state_split)
                else:
                    split(h, rec_hi[:, 0:n], rec_lo[:, 0:n], rec_hi_set, g.count(NR, RECURRENT.index(k) + 1), rec_split)

            def first_split(g):
                for c in range(NC):
                    dve.wait_ge(h2_ready, g.count(NC, c + 1))
                    split(half(h2, c), half(state_hi, c), half(state_lo, c), state_hi_set, g.count(NX, c + 1), state_split)

            def source(g, which, c):
                n = which * NC + c + 1
                dve.wait_ge(y_ps, g.count(2 * NC, n))
                wait_past(dve, y_lo_set, g.count(2 * NC, n - NC))
                wait_past(dve, agg_split, g.count(NC, c + 1 - (4 - which) * NC))
                sums = half(unsplit, c).rearrange("p (n d) -> p n d", d=P)
                dve.tensor_tensor(sums, small[c][:, :].rearrange("p (n d) -> p n d", d=P),
                                  bg[:, which, :].unsqueeze(1).broadcast_to([P, TPC, H]), ALU.add).then_inc(y_summed, 1)
                dve.wait_ge(y_summed, g.count(2 * NC, n))
                wait_past(dve, adj1_done if which == 0 else adj0_done, g.count(NC, 0 if which == 0 else NC))
                split(sums, tiles_of(y_hi, c), tiles_of(y_lo, c), y_hi_set, g.count(2 * NC, n), y_lo_set)

            def residual(g, c):
                dve.wait_ge(state_t, g.count(NC, c + 1))
                dve.tensor_tensor(tiles_of(xa[:, g.index], c), turn(g)[c][:, :].rearrange("p (n d) -> p n d", d=P),
                                  tiles_of(xa[:, g.index], c), ALU.add).then_inc(x1_ready, 1)

            def features(g, tiles, part):
                n = tiles.stop - tiles.start
                dve.wait_ge(ln_rstd[1], g.count(1, part))
                dve.tensor_tensor(scale[:, tiles], rstd[:, 1, tiles], dinv[:, tiles], ALU.mult).then_inc(ln_scaled, 1)
                dve.wait_ge(ln_scaled, g.count(1, part))
                dve.wait_ge(ln_centred[1], g.count(1, part))
                dve.scalar_tensor_tensor(out=norm[:, tiles, :], in0=norm[:, tiles, :], scalar=0.0,
                                         in1=scale[:, tiles].unsqueeze(2).broadcast_to([P, n, D]),
                                         op0=ALU.max, op1=ALU.mult).then_inc(f_scaled, 1)
                dve.wait_ge(f_scaled, g.count(1, part))
                wait_past(dve, agg_done, g.count(NC, 0))
                dve.tensor_copy(f_hi[:, tiles, :], norm[:, tiles, :]).then_inc(f_hi_set, 1)

            def features_lo(g, tiles, part):
                dve.wait_ge(f_hi_set, g.count(1, part))
                dve.tensor_tensor(f_lo[:, tiles, :], norm[:, tiles, :], f_hi[:, tiles, :].bitcast(F32),
                                  ALU.subtract).then_inc(f_lo_set, 1)

            def last_centred(g, c):
                tiles = slice(c * TPC, (c + 1) * TPC)
                dve.wait_ge(x1_ready, g.count(NC, c + 1))
                dve.wait_ge(ln_moments[1], g.count(1, 0))
                dve.wait_ge(ln_centred[1], g.count(1, 0))
                for n in range(c * TPC, (c + 1) * TPC):
                    ins = dve.bn_stats(stats[:, 1, n, :], xa[:, g.index, n, :])
                ins.then_inc(ln_stats[1], 1)
                dve.wait_ge(ln_stats[1], g.count(1, c + 1))
                for n in range(c * TPC, (c + 1) * TPC):
                    ins = dve.bn_aggr(moments[:, 1, n, :], stats[:, 1, n, :])
                ins.then_inc(ln_moments[1], 1)
                dve.wait_ge(ln_moments[1], g.count(1, c + 1))
                dve.tensor_tensor(veps[:, 1, tiles], moments[:, 1, tiles, 1], eps[:, tiles], ALU.add).then_inc(ln_veps[1], 1)
                dve.wait_ge(f_lo_set, g.count(1, 0))
                dve.wait_ge(f_t_ps, g.count(NC, 0))
                dve.tensor_tensor(norm[:, tiles, :], xa[:, g.index, tiles, :],
                                  moments[:, 1, tiles, 0].unsqueeze(2).broadcast_to([P, TPC, D]),
                                  ALU.subtract).then_inc(ln_centred[1], 1)

            def last_features(g, late):
                first, second = slice(0, TPC), slice(TPC, NT)
                residual(g, 0)
                last_centred(g, 0)
                residual(g, 1)
                features(g, first, 1)
                last_centred(g, 1)
                features(g, second, 2)
                scaled_aggregate(late, 1)
                features_lo(g, first, 1)
                features_lo(g, second, 2)

            def scaled_aggregate(g, c):
                dve.wait_ge(agg_done, g.count(NC, c + 1))
                wait_past(dve, y_lo_set, at_most(g.count(2 * NC, 6 * NC + c + 1), 2 * NC * B))
                wait_past(dve, agg_split, g.count(NC, c + 1 - NC))
                dve.wait_ge(f_t_set, g.count(NC, c + 1))
                dve.tensor_tensor(half(unsplit, c), agg_bank(g, c)[:, :], half(f_t, c), ALU.add).then_inc(agg_summed, 1)
                dve.wait_ge(agg_summed, g.count(NC, c + 1))
                dve.tensor_tensor(half(unsplit, c), half(unsplit, c), half(dinv_row, c), ALU.mult).then_inc(agg_scaled, 1)
                dve.wait_ge(agg_scaled, g.count(NC, c + 1))
                wait_past(dve, hid_ps, g.count(4, 0))
                split(half(unsplit, c), half(agg_hi, c), half(agg_lo, c), agg_hi_set, g.count(NC, c + 1), agg_split)

            def hidden_stats(g, pieces=range(4)):
                for n in pieces:
                    c, m = n // 2, n % 2
                    dve.wait_ge(hid_set, g.count(4, n + 1))
                    fence(n)
                    at = g.base * NC + c if g.loop is None else g.loop * NC + (g.base * NC + c)
                    dve.bn_stats(hstats[:, m, at, :], hidden_piece(g, n)).then_inc(hid_stats, 1)

            def split_weights():
                split(w1_stage, w1_hi[:, :], w1_lo[:, :], w1_hi_set, 1, w1_split)
                dve.tensor_tensor(bias[:, :], bias_in[:, 0, :], bias_in[:, 1, :], ALU.add).then_inc(consts_made, 1)
                for n, (lo, stage_, hi) in enumerate(
                        [(wih_lo[:, p, :], wih_stage[p], wih_hi[:, p, :]) for p in range(MAX_SKIP)]
                        + [(whh_lo[:, p, :], whh_stage[p], whh_hi[:, p, :]) for p in range(MAX_SKIP - 1)]):
                    dve.wait_ge(w_hi_ready, n + 1)
                    dve.tensor_tensor(lo, stage_, hi.bitcast(F32), ALU.subtract).then_inc(w_lo_ready, 1)
                dve.wait_ge(w_lo_ready, 2 * MAX_SKIP - 1)

            def stage(coming, front, lstm, ended, back, late):
                start = front is not None and front.loop is None and front.base == 0
                second = front is not None and front.loop is None and front.base == 1
                third = front is not None and front.loop is None and front.base == 2
                alone = lstm is None and not start
                for k in range(NS):
                    if lstm is not None:
                        cells(lstm, k)
                    if k == NS - 1 and front is not None:
                        first_split(front)
                    if lstm is not None:
                        states(lstm, k)
                    if k == 1 and ended is not None and not alone:
                        residual(ended, 0)
                        residual(ended, 1)
                    if k in (1, 2) and front is not None:
                        source(front, 0, k - 1)
                        if start and k == 2:
                            split_adjacency(range(EARLY_TILES, NT))
                            diagonal()
                    if k == 2 and back is not None:
                        scaled_aggregate(back, 0)
                    if k == 3 and ended is not None and not alone:
                        ln_moments_of(ended, 1)
                    if k == (3 if front is not None else 4) and back is not None:
                        scaled_aggregate(back, 1)
                    if k in (2, 3) and second:
                        masked_row_sums(k - 2)
                    if k == 3 and second:
                        degrees()
                    if k == 4 and second:
                        inverse_roots()
                    if k == 2 and third:
                        inverse_root_row()
                    if k == 4 and start:
                        dve.wait_ge(consts_in, 16 * (CONSTS - FIRST_CONSTS))
                    if k == 7 and start:
                        split_weights()
                    if k == (4 if front is not None else 5) and ended is not None and not alone:
                        features(ended, slice(0, NT), 1)
                    if k == (4 if front is not None else 6) and ended is not None and not alone:
                        features_lo(ended, slice(0, NT), 1)
                    if front is not None and k == (5 if back is not None else 6):
                        source(front, 1, 0)
                    if front is not None and k == 6:
                        source(front, 1, 1)
                    if k == (9 if front is not None else 8) and back is not None:
                        hidden_stats(back)
                    if k == (6 if start else 7) and coming is not None:
                        if start:
                            dve.wait_ge(x_second_in, 16)
                        if second:
                            dve.wait_ge(x_rest_in, 16 * (B - 2))
                        ln_moments_of(coming, 0)
                    if k == 9 and late is not None and not alone:
                        scaled_aggregate(late, 0)
                if alone:
                    last_features(ended, late)
                    hidden_stats(late)
                    scaled_aggregate(ended, 0)
                    scaled_aggregate(ended, 1)
                    hidden_stats(ended)
            periods(dve, stage)

            def batchnorm(which, all_stats, weights, ready):
                w = len(all_stats)
                for m in range(w):
                    ins = dve.bn_aggr(bnm[:, m, :], all_stats[m])
                ins.then_inc(bn_own, 1)
                dve.wait_ge(bn_own, 3 * which + 1)
                dve.tensor_scalar(bnv[:, :], bnm[:, :, 1], EPS, None, ALU.add).then_inc(bn_step, 1)
                dve.wait_ge(bn_rstd, which + 1)
                dve.tensor_tensor(bns[:, 0:w], bnr[:, 0:w], weights[:, 1, :], ALU.mult).then_inc(bn_own, 1)
                dve.wait_ge(bn_own, 3 * which + 2)
                dve.tensor_tensor(bnu[:, 0:w], bnm[:, 0:w, 0], bns[:, 0:w], ALU.mult).then_inc(bn_own, 1)
                dve.wait_ge(bn_own, 3 * which + 3)
                dve.tensor_tensor(bnt[:, 0:w], weights[:, 2, :], bnu[:, 0:w], ALU.subtract).then_inc(ready, 1)

            dve.wait_ge(hid_stats, 4 * B)
            batchnorm(0, [hstats[:, m, :, :].rearrange("p n s -> p (n s)") for m in range(2)], bn1, bn1_ready)
            for n in range(B * NC):
                dve.wait_ge(z_ps, n + 1)
                piece = z[:, W2_ORDER[n // NC], (n % NC) * CH:(n % NC + 1) * CH]
                dve.tensor_scalar(piece, gate_ps[n % 4][:, :], bn2[:, 0, 0:1], None, ALU.add).then_inc(z_set, 1)
                dve.wait_ge(z_set, n + 1)
                dve.bn_stats(zstats[:, n, :], piece).then_inc(z_stats, 1)
            dve.wait_ge(z_stats, B * NC)
            batchnorm(1, [zstats[:, :, :].rearrange("p n s -> p (n s)")], bn2, bn2_ready)

            with dve.Fori(0, B // 2) as i:
                pair = Graph(0, i)
                for n in range(OUT_SLOTS):
                    dve.wait_ge(y_t, pair.count(OUT_SLOTS, n + 1))
                    x1_half = xa_pairs[:, pair.index, n, :, :]
                    dve.tensor_tensor(x1_half, out_ps[n][:, :].rearrange("p (n d) -> p n d", d=P), x1_half,
                                      ALU.add).then_inc(y_added, 1)

        @block.tensor
        def _(pe):
            def product(bank, left, right, first=True, last=True):
                (a_hi, a_lo), (b_hi, b_lo) = left, right
                pe.matmul(bank, a_hi, b_hi, start=first, stop=False)
                pe.matmul(bank, a_hi, b_lo, start=False, stop=False)
                return pe.matmul(bank, a_lo, b_hi, start=False, stop=last)

            def step(g, k):
                st = STEPS[k]
                n = st.windows
                wait_past(pe, state_split, g.count(NX, state_ready(k)))
                for q in st.gates:
                    wait_past(pe, gate_read, g.count(NG, gate_freed(k, q)))
                    if k == 8 and q == FORGET:
                        wait_past(pe, hid_set, g.count(4, 4 - 2 * 4))
                    if k == NC + 1 and q == FORGET:
                        wait_past(pe, x1_ready, g.count(NC, 1 - NC))
                    at = slice(q * H, (q + 1) * H)
                    last = product(gate_ps[q][:, 0:n], (wih_hi[:, st.p - 1, at], wih_lo[:, st.p - 1, at]),
                                   (st.columns(state_hi), st.columns(state_lo)), last=st.zero_state)
                    if st.zero_state:
                        last.then_inc(gate_done, 1)
                if not st.zero_state:
                    pe.wait_ge(rec_split, g.count(NR, RECURRENT.index(k - 1) + 1))
                    for q in st.gates:
                        at = slice(q * H, (q + 1) * H)
                        product(gate_ps[q][:, 0:n], (whh_hi[:, st.p - 2, at], whh_lo[:, st.p - 2, at]),
                                (rec_hi[:, 0:n], rec_lo[:, 0:n]), first=False).then_inc(gate_done, 1)

            def transposed(banks, c, tile):
                for i in range(TPC):
                    last = pe.transpose(banks[c][:, i * P:(i + 1) * P], tile(c * TPC + i), ident[:, :])
                return last

            def norm_transposed(g):
                pe.wait_ge(ln_done, g.count(1, 1))
                for c in range(NC):
                    wait_past(pe, y_summed, g.count(2 * NC, c + 1 - NC))
                    if c == 0:
                        wait_past(pe, hid_set, g.count(4, 3 - 4 * 4))
                    transposed(small, c, lambda n: norm[:, n, :]).then_inc(norm_t, 1)

            def state_transposed(g):
                pe.wait_ge(h_ready, g.count(NS, NS))
                for c in range(NC):
                    if c == 1 and (g.loop is not None or g.base < B - 1):
                        pe.wait_ge(h2_ready, at_most(g.count(NC, NC + c + 1), B * NC))
                    transposed(turn(g), c, lambda n: state[:, n * P:(n + 1) * P]).then_inc(state_t, 1)

            def linear(g, which, c):
                if which == 0:
                    pe.wait_ge(feat0, g.count(NC, c + 1))
                else:
                    pe.wait_ge(feat1, g.count(NC, c + 1))
                    pe.wait_ge(y_summed, g.count(2 * NC, c + 1))
                    wait_past(pe, f_t_set, g.count(NC, c + 1 - 2 * NC))
                for i in range(TPC):
                    n = c * TPC + i
                    last = pe.matmul(small[c][:, i * P:(i + 1) * P], feat[:, n * P:(n + 1) * P], wg[:, which, :],
                                     start=True, stop=True)
                last.then_inc(y_ps, 1)

            def aggregate_hi(c, hi, tiles):
                for n in tiles:
                    pe.matmul(acc[c][:, :], hi[:, n, :], adj_hi[:, n, c * CH:(c + 1) * CH], start=n == 0, stop=False)
                    pe.matmul(acc[c][:, :], hi[:, n, :], adj_lo[:, n, c * CH:(c + 1) * CH], start=False, stop=False)

            def aggregate_lo(c, lo, tiles, bank):
                for n in tiles:
                    last = pe.matmul(bank[:, :], lo[:, n, :], adj_hi[:, n, c * CH:(c + 1) * CH], start=False,
                                     stop=n == NT - 1)
                return last

            def features_transposed(g, front):
                pe.wait_ge(f_scaled, g.count(1, NC if is_last(g) else 1))
                for c in range(NC):
                    if is_last(g):
                        bank = turn(g)[c]
                        pe.wait_ge(x1_ready, g.count(NC, c + 1))
                    else:
                        bank = small[c]
                        if front is not None:
                            pe.wait_ge(y_summed, front.count(2 * NC, c + 1))
                        else:
                            pe.wait_ge(hid_set, g.count(4, c - 1))
                    for i in range(TPC):
                        last = pe.transpose(bank[:, i * P:(i + 1) * P], norm[:, c * TPC + i, :], ident[:, :])
                    last.then_inc(f_t_ps, 1)

            def bank_free(g, which, c):
                if which == 0:
                    wait_past(pe, agg_scaled, g.count(NC, c + 1 - 3 * NC))
                    wait_past(pe, h2_ready, g.count(NC, c + 1 - NC))
                    if c == 1:
                        wait_past(pe, x1_ready, g.count(NC, c + 1 - 2 * NC))
                    if g.loop is None and g.base == 1:
                        pe.wait_ge(deg_step, NT + 2 + c)
                else:
                    pe.wait_ge(feat1, g.count(NC, c + 1))
                    wait_past(pe, hid_set, g.count(4, c + 1 - 3 * 4))

            def convolution_hi(g, which, c, tiles=ALL_TILES):
                if 0 in tiles:
                    bank_free(g, which, c)
                for part in range(NC):
                    of_part = [n for n in tiles if n // TPC == part]
                    if of_part:
                        pe.wait_ge(y_hi_set, g.count(2 * NC, which * NC + part + 1))
                        aggregate_hi(c, y_hi, of_part)

            def first_convolution_hi():
                for n in range(NT):
                    pe.wait_ge(y_hi_set, n // TPC + 1)
                    pe.wait_ge(adj_lo_ready, n + 1)
                    for c in range(NC):
                        aggregate_hi(c, y_hi, [n])

            def convolution_lo(g, which, c, tiles=ALL_TILES):
                pe.wait_ge(y_lo_set, g.count(2 * NC, which * NC + NC))
                last = aggregate_lo(c, y_lo, tiles, acc[c])
                if NT - 1 in tiles:
                    last.then_inc(adj0_done if which == 0 else adj1_done, 1)

            def last_hi(half_tiles, part, chunks):
                pe.wait_ge(f_hi_set, B - 1 + part)
                for n in half_tiles:
                    for c in chunks:
                        bank = agg_bank(Graph(B - 1), c)
                        pe.matmul(bank[:, :], f_hi[:, n, :], adj_hi[:, n, c * CH:(c + 1) * CH], start=n == 0, stop=False)
                        pe.matmul(bank[:, :], f_hi[:, n, :], adj_lo[:, n, c * CH:(c + 1) * CH], start=False, stop=False)

            def last_lo(c):
                pe.wait_ge(f_lo_set, B - 1 + NC)
                aggregate_lo(c, f_lo, ALL_TILES, agg_bank(Graph(B - 1), c)).then_inc(agg_done, 1)

            def normalised_hi(g, c, ended=None, tiles=ALL_TILES):
                if 0 in tiles:
                    pe.wait_ge(f_hi_set, g.count(1, 1))
                    wait_past(pe, h2_ready, at_most(g.count(NC, 2 * NC + c + 1), B * NC))
                    wait_past(pe, agg_scaled, g.count(NC, c + 1 - NC))
                    if c == 1 and ended is not None:
                        pe.wait_ge(x1_ready, ended.count(NC, c + 1))
                aggregate_hi(c, f_hi, tiles)

            def normalised_lo(g, c):
                pe.wait_ge(f_lo_set, g.count(1, 1))
                aggregate_lo(c, f_lo, ALL_TILES, acc[c]).then_inc(agg_done, 1)

            def hidden(g, n, front):
                c, m = n // 2, n % 2
                pe.wait_ge(agg_split, g.count(NC, c + 1))
                if front is None:
                    pe.wait_ge(hid_set, g.count(4, n - 1))
                elif n < 2:
                    pe.wait_ge(feat1, front.count(NC, n + 1))
                elif n == 2:
                    pe.wait_ge(y_summed, front.count(2 * NC, NC + 1))
                else:
                    pe.wait_ge(gate_read, g.count(NG, 2 * NG + gate_used(6, FORGET)))
                product(hid_bank(n, front)[:, :], (w1_hi[:, m * P:(m + 1) * P], w1_lo[:, m * P:(m + 1) * P]),
                        (agg_hi[:, c * CH:(c + 1) * CH], agg_lo[:, c * CH:(c + 1) * CH])).then_inc(hid_ps, 1)

            def row_sums(c, tiles):
                pe.wait_ge(h2_ready, c + 1)
                for n in tiles:
                    pe.matmul(acc[c][:, :], ones_r[:, :], adj_hi[:, n, c * CH:(c + 1) * CH], start=n == 0, stop=False)
                    last = pe.matmul(acc[c][:, :], ones_r[:, :], adj_lo[:, n, c * CH:(c + 1) * CH], start=False,
                                     stop=n == NT - 1)
                if NT - 1 in tiles:
                    last.then_inc(rowsum_ps, 1)

            def spread_inverse_roots(c):
                pe.wait_ge(dinv_step, 3)
                pe.wait_ge(h2_ready, NC + c + 1)
                if c == 1:
                    pe.wait_ge(x1_ready, c + 1)
                pe.matmul(acc[c][:, :], ones[:, :], spread[:, c * CH:(c + 1) * CH], start=True, stop=True).then_inc(dinv_ps, 1)

            def stage(coming, front, lstm, ended, back, late):
                start = front is not None and front.loop is None and front.base == 0
                second = front is not None and front.loop is None and front.base == 1
                third = front is not None and front.loop is None and front.base == 2
                for k in range(NS):
                    if k == 0 and front is not None:
                        norm_transposed(front)
                    if lstm is not None:
                        step(lstm, k)
                    if k == 0 and ended is not None:
                        state_transposed(ended)
                    if k == 1:
                        if back is not None:
                            normalised_hi(back, 0, ended)
                        if front is not None:
                            linear(front, 0, 0)
                            linear(front, 0, 1)
                    if second and k == 1:
                        row_sums(0, ALL_TILES)
                    if second and k in (2, 3):
                        row_sums(1, FIRST_TILES if k == 2 else LAST_TILES)
                    if k in (1, 2) and third:
                        spread_inverse_roots(k - 1)
                    if k == 2 and back is not None:
                        normalised_lo(back, 0)
                    if k == (2 if front is not None else 3) and back is not None:
                        normalised_hi(back, 1, ended)
                    if k == (3 if front is not None else 4) and back is not None:
                        normalised_lo(back, 1)
                    if k == 3:
                        if third:
                            pe.wait_ge(dinv_ready, NC)
                        if start:
                            first_convolution_hi()
                        elif front is not None:
                            convolution_hi(front, 0, 0)
                    if k == 4 and front is not None:
                        convolution_lo(front, 0, 0)
                        if not start:
                            convolution_hi(front, 0, 1)
                    if k == (5 if front is not None else 7) and ended is not None and lstm is not None:
                        features_transposed(ended, front)
                    if k == 5 and front is not None:
                        convolution_lo(front, 0, 1, ALL_TILES if back is not None else FIRST_TILES)
                    if k == 6 and front is not None and back is None:
                        convolution_lo(front, 0, 1, LAST_TILES)
                        if start:
                            pe.wait_ge(consts_in, 16 * (CONSTS - FIRST_CONSTS))
                    if front is not None and k == (5 if back is not None else 6):
                        linear(front, 1, 0)
                    if front is not None and k == 6:
                        linear(front, 1, 1)
                    if back is not None and front is not None and k == 6:
                        for n in range(4):
                            hidden(back, n, front)
                    if back is not None and front is None and k in (5, 6):
                        for n in range(2 * (k - 5), 2 * (k - 5) + 2):
                            hidden(back, n, front)
                    if k == 7 and front is not None:
                        convolution_hi(front, 1, 0)
                    if k == 8 and front is not None:
                        convolution_lo(front, 1, 0)
                        convolution_hi(front, 1, 1, range(2))
                    if k == 9 and front is not None:
                        convolution_hi(front, 1, 1, range(2, NT))
                    if k == 10 and front is not None:
                        convolution_lo(front, 1, 1)
                    if late is not None and lstm is not None:
                        if k == 6:
                            normalised_hi(late, 0, tiles=FIRST_TILES)
                        if k == 7:
                            normalised_hi(late, 0, tiles=LAST_TILES)
                        if k == 8:
                            normalised_lo(late, 0)
                        if k == 9:
                            normalised_hi(late, 1, tiles=FIRST_TILES)
                        if k == 10:
                            normalised_hi(late, 1, tiles=LAST_TILES)
                if late is not None and lstm is None:
                    normalised_lo(late, 1)
                    pe.wait_ge(f_t_set, NC * (B - 1))
                    hidden(late, 0, front)
                    hidden(late, 1, front)
                    last_hi(FIRST_TILES, 1, range(NC))
                    last_hi(LAST_TILES, 2, [0])
                    features_transposed(ended, front)
                    hidden(late, 2, front)
                    hidden(late, 3, front)
                    last_lo(0)
                    last_hi(LAST_TILES, 2, [1])
                    last_lo(1)
                    for n in range(4):
                        hidden(ended, n, front)
                if start:
                    pe.wait_ge(consts_made, 1)
                    pe.wait_ge(w1_split, 1)
                    pe.wait_ge(w_lo_ready, 2 * MAX_SKIP - 1)
            def stay_awake(rounds):
                with pe.Fori(0, rounds) as _:
                    for _n in range(4):
                        pe.matmul(gate_ps[0][:, 0:P], ones[:, :], ones[:, :], start=True, stop=True)

            pe.wait_ge(consts_set, 6)
            stay_awake(7)
            pe.wait_ge(first_consts_in, 16 * FIRST_CONSTS)
            periods(pe, stage)

            stay_awake(4)
            for n in range(B * NC):
                b, c = W2_ORDER[n // NC], n % NC
                if n >= 4:
                    pe.wait_ge(z_set, n - 3)
                for m in range(2):
                    pe.wait_ge(hid_relu, 2 * n + m + 1 if n < NC else 4 + 2 * (n // NC - 1) + m + 1)
                    last = pe.matmul(gate_ps[n % 4][:, :], w2[:, m, :], hidden_layer(b)[:, c, m, :],
                                     start=m == 0, stop=m == 1)
                last.then_inc(z_ps, 1)

            def output(pair):
                for n in range(OUT_SLOTS):
                    pe.wait_ge(y_set, pair.count(OUT_SLOTS, n + 1))
                    wait_past(pe, y_added, pair.count(OUT_SLOTS, n + 1 - OUT_SLOTS))
                    transposed(out_ps, n, lambda i: out_slot[n][:, i % TPC * P:(i % TPC + 1) * P]).then_inc(y_t, 1)
            output(Graph(0))
            with pe.Fori(0, B // 2 - 1) as i:
                output(Graph(1, i))


def kernel(x, adj, L0_gnn_Wg0, L0_gnn_bg0, L0_gnn_Wg1, L0_gnn_bg1, L0_gnn_Wih, L0_gnn_Whh, L0_gnn_bih, L0_gnn_bhh,
           L1_gnn_W1, L1_gnn_b1, L1_gnn_g1, L1_gnn_be1, L1_gnn_W2, L1_gnn_b2, L1_gnn_g2, L1_gnn_be2):
    import numpy as np
    import concourse.bacc as bacc
    from concourse.bass_utils import run_bass_kernel_spmd

    def gate_weights(w):
        return w.transpose(2, 0, 1)

    def gate_bias(b):
        return b.reshape(MAX_SKIP * GATES, H).T

    laid = dict(
        x=x, adj_t=adj.T, wg0=L0_gnn_Wg0, wg1=L0_gnn_Wg1, bg0=L0_gnn_bg0[None, :], bg1=L0_gnn_bg1[None, :],
        wih_t=gate_weights(L0_gnn_Wih), whh_t=gate_weights(L0_gnn_Whh), bih_t=gate_bias(L0_gnn_bih),
        bhh_t=gate_bias(L0_gnn_bhh), w1_t=L1_gnn_W1.T, b1_t=L1_gnn_b1.reshape(2, P).T, g1_t=L1_gnn_g1.reshape(2, P).T,
        be1_t=L1_gnn_be1.reshape(2, P).T, w2_t=L1_gnn_W2.T.reshape(2, P, D).transpose(1, 0, 2),
        b2_t=L1_gnn_b2[:, None], g2_t=L1_gnn_g2[:, None], be2_t=L1_gnn_be2[:, None], ident_in=np.eye(P, dtype=np.float32))
    nc = bacc.Bacc("TRN2", target_bir_lowering=False, num_devices=1, dynamic_dma_scratch_size=1024)
    arrays, args = {}, {}
    for name, a in laid.items():
        a = np.ascontiguousarray(a)
        arrays[f"{name}_dram"] = a
        args[name] = nc.dram_tensor(f"{name}_dram", a.shape, mybir.dt.from_np(a.dtype), kind="ExternalInput").ap()
    out = nc.dram_tensor("out_dram", (B, T, D), F32, kind="ExternalOutput").ap()
    program(nc, out=out, **args)
    r = run_bass_kernel_spmd(nc, [arrays], core_ids=[0])
    return r.results[0]["out_dram"]
```
